# Optimizing a Trainium2 kernel written in Bass

```python
import numpy as np
import jax
import jax.numpy as jnp

def _softmax(x, axis=-1):
    return jax.nn.softmax(x, axis=axis)

def _gelu(x):
    return jax.nn.gelu(x, approximate=True)

def _silu(x):
    return jax.nn.silu(x)

def _sigmoid(x):
    return jax.nn.sigmoid(x)

def _layernorm(x, axis=-1, eps=1e-05):
    m = jnp.mean(x, axis=axis, keepdims=True)
    v = jnp.var(x, axis=axis, keepdims=True)
    return (x - m) / jnp.sqrt(v + eps)

def _scatter_add(tgt, idx, src, axis=0):
    return tgt.at[idx].add(src)

def _segment_sum(src, seg, n):
    return jax.ops.segment_sum(src, seg, n)
kernel_name = 'mk_adj_ffn_d1_adj_r2_e6e06a'

def setup_inputs(seed: int=0):
    np.random.seed(seed)
    _w = jnp.asarray

    def _rec_inputs():
        import jax
        import jax.numpy as jnp
        _gk = jax.random.key(seed)
        x = -0.0002928 + 1 * jax.random.normal(jax.random.fold_in(_gk, 1), (128, 64, 128), jnp.float32)
        _a = jax.random.bernoulli(jax.random.fold_in(_gk, 2), 0.125, (128, 64, 64))
        _a = jnp.logical_or(_a, jnp.swapaxes(_a, -1, -2))
        _a = jnp.logical_or(_a, jnp.eye(64, dtype=bool))
        _af = _a.astype(jnp.float32)
        _af = _af * jax.random.uniform(jax.random.fold_in(_gk, 3), (128, 64, 64), jnp.float32, 0.05, 1)
        adj = _af
        return (x, adj)
    x, adj = _rec_inputs()

    def _L0_gnn_setup():
        import jax, jax.numpy as jnp
        import numpy as np
        B, N, D, H = (8, 1024, 128, 512)
        RMS_EPS = 1e-06

        def _rmsnorm(h, w, eps=RMS_EPS):
            var = jnp.mean(jnp.square(h), axis=-1, keepdims=True)
            return h * jax.lax.rsqrt(var + eps) * w
        key = jax.random.key(seed)
        ks = jax.random.split(key, 5)
        x = jax.random.normal(ks[0], (B, N, D), dtype=jnp.float32)
        adjacency = jax.random.uniform(ks[1], (B, N, N), dtype=jnp.float32)
        epsilon = jnp.zeros((), dtype=jnp.float32)
        W1 = jax.random.normal(ks[2], (D, H), dtype=jnp.float32) * (1.0 / np.sqrt(D))
        b1 = jnp.zeros((H,), dtype=jnp.float32)
        rms_weight = jnp.ones((H,), dtype=jnp.float32)
        W2 = jax.random.normal(ks[3], (H, D), dtype=jnp.float32) * (1.0 / np.sqrt(H))
        b2 = jnp.zeros((D,), dtype=jnp.float32)
        return {'x': x, 'adjacency': adjacency, 'epsilon': epsilon, 'W1': W1, 'b1': b1, 'rms_weight': rms_weight, 'W2': W2, 'b2': b2}
    _L0_gnn_all = _L0_gnn_setup()
    _L0_gnn_in = {k: v for k, v in _L0_gnn_all.items() if k in ('epsilon', 'W1', 'b1', 'rms_weight', 'W2', 'b2')}
    del _L0_gnn_all

    def _L0_ffn_setup():
        import jax, jax.numpy as jnp
        import numpy as np
        TOP_K = 2
        key = jax.random.key(seed)
        ks = jax.random.split(key, 4)
        B, L, D, H, E = (8, 2048, 128, 512, 8)
        s = 0.02
        return {'x': jax.random.normal(ks[0], (B, L, D), jnp.float32), 'Wg': jax.random.normal(ks[1], (D, E), jnp.float32) * s, 'bg': jnp.zeros((E,), jnp.float32), 'W1': jax.random.normal(ks[2], (E, D, H), jnp.float32) * s, 'b1': jnp.zeros((E, H), jnp.float32), 'W2': jax.random.normal(ks[3], (E, H, D), jnp.float32) * s, 'b2': jnp.zeros((E, D), jnp.float32)}
    _L0_ffn_all = _L0_ffn_setup()
    _L0_ffn_in = {k: v for k, v in _L0_ffn_all.items() if k in ('Wg', 'bg', 'W1', 'b1', 'W2', 'b2')}
    del _L0_ffn_all
    return {'x': x, 'adj': adj, 'L0_gnn_epsilon': _L0_gnn_in['epsilon'], 'L0_gnn_W1': _L0_gnn_in['W1'], 'L0_gnn_b1': _L0_gnn_in['b1'], 'L0_gnn_rms_weight': _L0_gnn_in['rms_weight'], 'L0_gnn_W2': _L0_gnn_in['W2'], 'L0_gnn_b2': _L0_gnn_in['b2'], 'L0_ffn_Wg': _L0_ffn_in['Wg'], 'L0_ffn_bg': _L0_ffn_in['bg'], 'L0_ffn_W1': _L0_ffn_in['W1'], 'L0_ffn_b1': _L0_ffn_in['b1'], 'L0_ffn_W2': _L0_ffn_in['W2'], 'L0_ffn_b2': _L0_ffn_in['b2']}

def reference(x, adj, L0_gnn_epsilon, L0_gnn_W1, L0_gnn_b1, L0_gnn_rms_weight, L0_gnn_W2, L0_gnn_b2, L0_ffn_Wg, L0_ffn_bg, L0_ffn_W1, L0_ffn_b1, L0_ffn_W2, L0_ffn_b2):
    import jax
    import jax.numpy as jnp

    def _L0_gnn_ref(x, adjacency, epsilon, W1, b1, rms_weight, W2, b2):
        import jax, jax.numpy as jnp
        import numpy as np
        B, N, D, H = (8, 1024, 128, 512)
        RMS_EPS = 1e-06

        def _rmsnorm(h, w, eps=RMS_EPS):
            var = jnp.mean(jnp.square(h), axis=-1, keepdims=True)
            return h * jax.lax.rsqrt(var + eps) * w
        neighbor_sum = jnp.einsum('bnm,bmd->bnd', adjacency, x)
        agg = epsilon * x + neighbor_sum
        h = jnp.einsum('bnd,dh->bnh', agg, W1) + b1
        h = jax.nn.silu(_rmsnorm(h, rms_weight))
        out = jnp.einsum('bnh,hd->bnd', h, W2) + b2
        return out

    def _L0_ffn_ref(x, Wg, bg, W1, b1, W2, b2):
        import jax, jax.numpy as jnp
        import numpy as np
        TOP_K = 2
        B, L, D = x.shape
        E = W1.shape[0]
        xf = x.reshape(-1, D)
        gate_logits = xf @ Wg + bg
        top_w, top_i = jax.lax.top_k(gate_logits, TOP_K)
        top_w = jax.nn.softmax(top_w, axis=-1)
        w_dense = jnp.sum(jax.nn.one_hot(top_i, E, dtype=xf.dtype) * top_w[..., None], axis=1)
        out = jnp.zeros_like(xf)
        for e in range(E):
            h = jax.nn.gelu(xf @ W1[e] + b1[e], approximate=False)
            out = out + w_dense[:, e:e + 1] * (h @ W2[e] + b2[e])
        return out.reshape(B, L, D)
    x = x + _L0_gnn_ref(_layernorm(x, axis=-1), adj, L0_gnn_epsilon, L0_gnn_W1, L0_gnn_b1, L0_gnn_rms_weight, L0_gnn_W2, L0_gnn_b2)
    x = x + _L0_ffn_ref(_layernorm(x, axis=-1), L0_ffn_Wg, L0_ffn_bg, L0_ffn_W1, L0_ffn_b1, L0_ffn_W2, L0_ffn_b2)
    return x

_drawn_inputs = setup_inputs


def setup_inputs(seed=0):
    import zlib

    import numpy as np

    out = dict(_drawn_inputs(seed))
    spreads = {'L0_gnn_b1': (0.0, 0.295),
     'L0_gnn_rms_weight': (1.0, 0.2),
     'L0_gnn_b2': (0.0, 0.1),
     'L0_ffn_bg': (0.0, 0.1),
     'L0_ffn_b1': (0.0, 0.566),
     'L0_ffn_b2': (0.0, 0.1)}
    factors = {}
    for name, (base, spread) in spreads.items():
        noise = np.random.default_rng([zlib.crc32(name.encode()), seed]).standard_normal(out[name].shape)
        drawn = base * np.exp(spread * noise) if base else spread * noise
        out[name] = jnp.asarray(drawn.astype(out[name].dtype))
    for name, factor in factors.items():
        out[name] = (out[name] * factor).astype(out[name].dtype)
    return out
```

```python
from contextlib import ExitStack

import numpy as np

import concourse.bass as bass
from concourse import mybir

F32 = mybir.dt.float32
BF16 = mybir.dt.bfloat16
I32 = mybir.dt.int32
U32 = mybir.dt.uint32
ALU = mybir.AluOpType
ACT = mybir.ActivationFunctionType
AX = mybir.AxisListType

P = 128
JT = 4
GROUP = JT * P
SLOTS = 256
HT = SLOTS // P
TOP_K = 2
LN_EPS = 1e-5
RMS_EPS = 1e-6

TOKEN, WEIGHT, ROW = P, P + 1, P + 3


class Chain:

    def __init__(self, engine, sem, done):
        self.engine, self.sem, self.done, self.n = engine, sem, done, 0

    def link(self, instruction, wait=None):
        self.n += 1
        instruction.then_inc(self.sem, 1)
        if wait:
            wait(self.engine, self.sem, self.done + self.n)
        else:
            self.engine.wait_ge(self.sem, self.done + self.n)


def moe_gnn(nc, x, adj_t, epsilon, g_w1, vectors, g_w2, f_wg, f_bg, f_w1, f_w2, f_b2, out):
    T, D = x.shape
    H = g_w1.shape[1]
    E = f_wg.shape[1]
    NODES = adj_t.shape[1]
    C = H // P
    G = T // GROUP
    BPT = P // NODES
    KE = TOP_K * E
    REGION = T + SLOTS
    DUMMY = KE * REGION
    TILES = (T + E * (SLOTS - 1)) // SLOTS
    NT = TOP_K * TILES
    BLOCK = 2 * C * P + C + P
    OB1, OB2 = 2 * C * P, 2 * C * P + C
    NV = vectors.shape[0]
    GB1, GRW, GB2, FB1 = 0, C, 2 * C, 2 * C + 1
    assert D == P and C == 4 and BPT == 2 and G % 2 == 0 and TILES % 2 == 1 and HT == 2

    with ExitStack() as ctx:
        def sb(name, shape, dt=F32):
            return ctx.enter_context(nc.sbuf_tensor(name, shape, dt))

        def sem(name):
            return ctx.enter_context(nc.semaphore(name))

        rows = nc.dram_tensor("dispatched_rows", (DUMMY + SLOTS, ROW), F32).ap()

        ident = sb("ident", [P, P])
        eps_ident = sb("eps_ident", [P, P])
        ones = sb("ones", [P, P])
        ones_bf = sb("ones_bf", [P, P], BF16)
        before = sb("before", [P, P], BF16)
        neg_half = sb("neg_half", [P, JT])
        expert_no = sb("expert_no", [P, E])
        tile_no = sb("tile_no", [P, TILES])
        region_base = sb("region_base", [P, KE])
        token_no = sb("token_no", [P, JT], I32)
        pad_rows = sb("pad_rows", [P, HT, ROW])
        eps_col = sb("eps_col", [P, 1])
        bg_all = sb("bg_all", [P, E])
        w1g = sb("w1g", [P, H])
        w2g = sb("w2g", [P, C, P])
        wg = sb("wg", [P, E])
        vec_rows = sb("vec_rows", [NV, P])
        vec_cols = sb("vec_cols", [P, NV])
        experts = sb("experts", [P, E * BLOCK])

        xs = sb("xs", [P, G * JT, P])
        adj_blocks = sb("adj_blocks", [P, 2, JT, P])
        stats1 = sb("stats1", [P, JT, 6])
        stats2 = sb("stats2", [P, JT, 6])
        mv1 = sb("mv1", [P, JT, 2])
        mv2 = sb("mv2", [P, JT, 2])
        var1 = sb("var1", [P, JT])
        var2 = sb("var2", [P, JT])
        rstd1 = sb("rstd1", [P, JT])
        rstd2 = sb("rstd2", [P, JT])
        xn = sb("xn", [P, 2, JT, P])
        agg = sb("agg", [P, GROUP])
        squares = sb("squares", [P, C, GROUP])
        sq_pair = sb("sq_pair", [P, 2, GROUP])
        sq_sum = sb("sq_sum", [P, GROUP])
        mean_sq = sb("mean_sq", [P, JT])
        rrms = sb("rrms", [P, JT])
        rrms_diag = sb("rrms_diag", [P, JT, P])
        rrms_all = sb("rrms_all", [P, GROUP])
        normed = sb("normed", [P, C, GROUP])
        hidden = sb("hidden", [P, C, GROUP])
        gnn_t = sb("gnn_t", [P, GROUP])
        payload = sb("payload", [P, 2, JT, ROW])
        xn2_t = sb("xn2_t", [P, GROUP])
        logits = sb("logits", [P, JT, E])
        top_vals = sb("top_vals", [P, JT, 8])
        top_idx = sb("top_idx", [P, JT, 8], U32)
        top_no = sb("top_no", [P, JT, TOP_K])
        gap = sb("gap", [P, JT])
        half_tanh = sb("half_tanh", [P, JT])
        chosen = sb("chosen", [P, 2, JT * KE], BF16)
        next_row = sb("next_row", [P, KE])
        row_cand = sb("row_cand", [P, JT, KE])
        row_f = sb("row_f", [P, JT * TOP_K])
        row_idx = sb("row_idx", [P, 2, JT * TOP_K], I32)

        region_end = sb("region_end", [P, KE], I32)
        count_i = sb("count_i", [P, KE], I32)
        tiles_i = sb("tiles_i", [P, KE], I32)
        tiles_f = sb("tiles_f", [P, KE])
        zeros_e = sb("zeros_e", [P, E])
        tiles_cum = sb("tiles_cum", [P, KE])
        skip = sb("skip", [P, KE])
        passed = sb("passed", [P, TILES, E])
        skipped = sb("skipped", [P, TILES, E])
        tile_expert = sb("tile_expert", [P, TILES])
        tile_row = sb("tile_row", [P, TILES])
        over = sb("over", [P, TILES])
        expert_tab = sb("expert_tab", [P, NT], I32)
        row_tab = sb("row_tab", [P, NT], I32)

        slot_rows = sb("slot_rows", [P, 2, HT, ROW])
        slot_t = sb("slot_t", [P, 2, SLOTS])
        block_w = sb("block_w", [P, 2, BLOCK])
        gelu_t = sb("gelu_t", [P, 2, C, SLOTS])
        y_bias = sb("y_bias", [P, 2, HT, P])
        y_out = sb("y_out", [P, 2, HT, P])

        ps_h = ctx.enter_context(nc.psum_tensor("ps_h", [P, C, 512], F32))
        ps_a = ctx.enter_context(nc.psum_tensor("ps_a", [P, 512], F32))
        ps_b = ctx.enter_context(nc.psum_tensor("ps_b", [P, 512], F32))
        ps_c = ctx.enter_context(nc.psum_tensor("ps_c", [P, 512], F32))
        ps_d = ctx.enter_context(nc.psum_tensor("ps_d", [P, 512], F32))
        MS, LG, PR, TO = 0, 8, 64, 192

        consts_loaded = sem("consts_loaded")
        experts_loaded = sem("experts_loaded")
        pool_consts = sem("pool_consts")
        dve_consts = sem("dve_consts")
        vecs_turned = sem("vecs_turned")
        x_loaded = [sem(f"x_loaded{b}") for b in range(2)]
        adj_loaded = [sem(f"adj_loaded{b}") for b in range(2)]
        ln1_chain = sem("ln1_chain")
        var1_ready = sem("var1_ready")
        rstd1_ready = sem("rstd1_ready")
        xn_ready = sem("xn_ready")
        agg_done = sem("agg_done")
        agg_copied = sem("agg_copied")
        h_done = sem("h_done")
        squares_ready = sem("squares_ready")
        sq_chain = sem("sq_chain")
        sq_sum_ready = sem("sq_sum_ready")
        ms_done = sem("ms_done")
        ms_ready = sem("ms_ready")
        rrms_ready = sem("rrms_ready")
        diag_ready = sem("diag_ready")
        spread_done = sem("spread_done")
        spread_copied = sem("spread_copied")
        normed_ready = sem("normed_ready")
        hidden_ready = sem("hidden_ready")
        gnn_done = sem("gnn_done")
        gnn_copied = sem("gnn_copied")
        gnn_turned = sem("gnn_turned")
        x2_ready = sem("x2_ready")
        x2_stored = sem("x2_stored")
        ln2_chain = sem("ln2_chain")
        var2_ready = sem("var2_ready")
        rstd2_ready = sem("rstd2_ready")
        xn2_ready = sem("xn2_ready")
        xn2_turned = sem("xn2_turned")
        xn2_copied = sem("xn2_copied")
        logits_done = sem("logits_done")
        gate_chain = sem("gate_chain")
        gap_ready = sem("gap_ready")
        tanh_ready = sem("tanh_ready")
        chosen_ready = sem("chosen_ready")
        prefix_done = sem("prefix_done")
        prefix_read = sem("prefix_read")
        row_chain = sem("row_chain")
        rows_ready = sem("rows_ready")
        dispatched = [sem(f"dispatched{b}") for b in range(2)]
        table_chain = sem("table_chain")
        ends_ready = sem("ends_ready")
        padded = sem("padded")
        tables_ready = sem("tables_ready")
        slots_loaded = [sem(f"slots_loaded{b}") for b in range(2)]
        slots_turned = sem("slots_turned")
        slots_copied = sem("slots_copied")
        block_ready = sem("block_ready")
        fh_done = sem("fh_done")
        gelu_ready = sem("gelu_ready")
        y_done = sem("y_done")
        y_chain = sem("y_chain")
        y_ready = sem("y_ready")
        added = [sem(f"added{b}") for b in range(2)]

        def wait_apart(engine, semaphore, value):
            if not isinstance(value, int):
                value = engine.to_reg(value)
                engine.wait_ge(pool_consts, 1)
            engine.wait_ge(semaphore, value)

        def live(t, s):
            return not isinstance(t, int) or 0 <= t < G

        def steps(engine, step):
            for s in (0, 1):
                step(s, s % 2)
            with engine.Fori(1, G // 2 - 1) as pair:
                step(pair * 2, 0)
                step(pair * 2 + 1, 1)
            for s in range(G - 2, G + 2):
                step(s, s % 2)

        x_view = x.rearrange("(r p) d -> p r d", p=P)
        out_view = out.rearrange("(r p) d -> p r d", p=P)
        adj_view = adj_t.rearrange("(r h) m n -> h m r n", h=BPT)

        block = ctx.enter_context(nc.Block())

        @block.sync
        def _(sp):
            for dst, src in (
                (w1g[:], g_w1), (w2g[:], g_w2.rearrange("(c p) d -> p c d", p=P)),
                (wg[:], f_wg), (vec_rows[:], vectors),
                (eps_col[:], epsilon.to_broadcast([P, 1])), (bg_all[:], f_bg.to_broadcast([P, E])),
            ):
                sp.dma_start(dst, src).then_inc(consts_loaded, 16)

            def load_x(t, b):
                if not isinstance(t, int) or t >= 2:
                    sp.wait_ge(x_loaded[b], 8 * (t - b))
                sp.dma_start(xs[:, bass.ds(t * JT, JT), :],
                             x_view[:, bass.ds(t * JT, JT), :]).then_inc(x_loaded[b], 16)

            def load_adj(t, b):
                for h in range(BPT):
                    half = slice(h * NODES, (h + 1) * NODES)
                    sp.dma_start(adj_blocks[half, b, :, half],
                                 adj_view[h, :, bass.ds(t * JT, JT), :]).then_inc(adj_loaded[b], 16)

            load_x(0, 0)
            load_x(1, 1)
            sp.wait_ge(pool_consts, 1)
            load_adj(0, 0)
            load_adj(1, 1)
            for e in range(E):
                blk = experts[:, e * BLOCK:(e + 1) * BLOCK]
                sp.dma_start(blk[:, 0:H], f_w1[e]).then_inc(experts_loaded, 16)
                sp.dma_start(blk[:, H:2 * H].rearrange("p (c d) -> p c d", c=C),
                             f_w2[e].rearrange("(c p) d -> p c d", p=P)).then_inc(experts_loaded, 16)
                sp.dma_start(blk[:, OB2:OB2 + P],
                             f_b2[e:e + 1, :].to_broadcast([P, P])).then_inc(experts_loaded, 16)

            def step(s, b):
                if live(s + 2, s):
                    load_x(s + 2, b)
                    sp.wait_ge(agg_done, s + 1)
                    load_adj(s + 2, b)
                if live(s - 1, s):
                    sp.wait_ge(x2_ready, s)
                    sp.dma_start(out_view[:, bass.ds((s - 1) * JT, JT), :],
                                 xs[:, bass.ds((s - 1) * JT, JT), :]).then_inc(x2_stored, 16)

            steps(sp, step)

            sp.wait_ge(pool_consts, 3)
            sp.dma_start(rows[DUMMY:DUMMY + SLOTS, :].rearrange("(h p) c -> p h c", p=P),
                         pad_rows[:]).then_inc(padded, 16)
            sp.wait_ge(ends_ready, 1)
            for g in range(KE):
                end = sp.value_load(region_end[0:1, g:g + 1], min_val=0, max_val=DUMMY - SLOTS)
                sp.dma_start(rows[bass.ds(end, SLOTS), :].rearrange("(h p) c -> p h c", p=P),
                             pad_rows[:]).then_inc(padded, 16)

            def load_slots(i, b, first):
                if not first:
                    sp.wait_ge(added[b], 16 * HT * (i - b) // 2 if isinstance(i, int) else (i - b) * (8 * HT))
                start = sp.value_load(row_tab[0:1, bass.ds(i, 1)], min_val=0, max_val=DUMMY)
                sp.dma_start(slot_rows[:, b, :, :],
                             rows[bass.ds(start, SLOTS), :].rearrange("(h p) c -> p h c", p=P)
                             ).then_inc(slots_loaded[b], 16)

            sp.wait_ge(tables_ready, 1)
            sp.wait_ge(padded, 16 * (KE + 1))
            for b in range(2):
                sp.wait_ge(dispatched[b], 16 * JT * TOP_K * (G // 2))
            load_slots(0, 0, True)
            load_slots(1, 1, True)
            with sp.Fori(1, NT // 2) as pair:
                load_slots(pair * 2, 0, False)
                load_slots(pair * 2 + 1, 1, False)
            sp.wait_ge(x2_stored, 16 * G)
            for b in range(2):
                sp.wait_ge(added[b], 16 * HT * (NT // 2))

        @block.gpsimd
        def _(pool):
            pool.memset(adj_blocks[:], 0.0).then_inc(pool_consts, 1)
            pool.memset(ident[:], 0.0)
            pool.memset(before[:], 0.0)
            pool.memset(pad_rows[:], 0.0)
            pool.memset(neg_half[:], -0.5)
            pool.memset(ones[:], 1.0)
            pool.memset(ones_bf[:], 1.0)
            pool.iota(expert_no[:], [[1, E]], base=0, channel_multiplier=0,
                      allow_small_or_imprecise_dtypes=True)
            pool.iota(tile_no[:], [[1, TILES]], base=0, channel_multiplier=0,
                      allow_small_or_imprecise_dtypes=True)
            pool.iota(token_no[:], [[P, JT]], base=0, channel_multiplier=1)
            pool.iota(top_no[:, 0, 0:1], [[1, 1]], base=0, channel_multiplier=0,
                      allow_small_or_imprecise_dtypes=True).then_inc(pool_consts, 1)
            pool.wait_ge(pool_consts, 2)
            pool.memset(pad_rows[:, :, TOKEN:TOKEN + 1].bitcast(I32), T).then_inc(pool_consts, 1)
            pool.affine_select(out=ident[:], in_=ident[:], compare_op=ALU.not_equal, fill=1.0,
                               base=0, pattern=[[-1, P]], channel_multiplier=1)
            pool.affine_select(out=before[:], in_=before[:], compare_op=ALU.is_ge, fill=1.0,
                               base=0, pattern=[[-1, P]], channel_multiplier=1).then_inc(pool_consts, 1)

            def rsqrt1(t):
                pool.wait_ge(var1_ready, t + 1)
                if not isinstance(t, int) or t >= 1:
                    pool.wait_ge(xn_ready, t)
                pool.tensor_tensor(rstd1[:], var1[:], neg_half[:], ALU.pow).then_inc(rstd1_ready, 1)

            def step(s, b):
                if live(s, s):
                    pool.wait_ge(ms_ready, s + 1)
                    pool.tensor_tensor(rrms[:], mean_sq[:], neg_half[:],
                                       ALU.pow).then_inc(rrms_ready, 1)
                if live(s - 1, s):
                    pool.wait_ge(var2_ready, s)
                    pool.tensor_tensor(rstd2[:], var2[:], neg_half[:],
                                       ALU.pow).then_inc(rstd2_ready, 1)
                if live(s + 2, s):
                    rsqrt1(s + 2)
                if live(s - 2, s):
                    wait_apart(pool, rows_ready, s - 1)
                    for jk in range(JT * TOP_K):
                        pool.indirect_dma_start(
                            rows, bass.IndirectOffsetOnAxis(row_idx[:, b, jk:jk + 1], 0),
                            payload[:, b, jk // TOP_K, :], None).then_inc(dispatched[b], 16)

            rsqrt1(0)
            rsqrt1(1)
            steps(pool, step)

            def add_tile(i, b):
                wait_apart(pool, y_ready, i + 1)
                for h in range(HT):
                    pool.indirect_dma_start(
                        out, bass.IndirectOffsetOnAxis(slot_rows[:, b, h, TOKEN:TOKEN + 1].bitcast(I32), 0),
                        y_out[:, b, h, :], None, bounds_check=T - 1, oob_is_err=False,
                        compute_op=ALU.add).then_inc(added[b], 16)

            pool.wait_ge(x2_stored, 16 * G)
            for k in range(TOP_K):
                first = k * TILES
                if k:
                    pool.wait_ge(added[0], 16 * HT * ((TILES + 1) // 2))
                    pool.wait_ge(added[1], 16 * HT * (TILES // 2))
                add_tile(first, first % 2)
                with pool.Fori(0, TILES // 2) as pair:
                    add_tile(pair * 2 + (first + 1), (first + 1) % 2)
                    add_tile(pair * 2 + (first + 2), first % 2)

        @block.tensor
        def _(pe):
            pe.wait_ge(consts_loaded, 16 * 6)
            pe.wait_ge(pool_consts, 4)
            pe.transpose(ps_d[:, 0:NV], vec_rows[:], ident[0:NV, 0:NV]).then_inc(vecs_turned, 1)

            def aggregate(t, b):
                pe.wait_ge(adj_loaded[b], 16 * (t - b) + 32)
                pe.wait_ge(xn_ready, t + 1)
                if not isinstance(t, int) or t >= 1:
                    pe.wait_ge(agg_copied, t)
                if not isinstance(t, int) or t >= 2:
                    pe.wait_ge(x2_ready, t - 1)
                for j in range(JT):
                    cols = ps_b[:, j * P:(j + 1) * P]
                    pe.matmul(cols, xn[:, b, j, :], adj_blocks[:, b, j, :], start=True, stop=False)
                    mm = pe.matmul(cols, xn[:, b, j, :], eps_ident[:], start=False, stop=True)
                mm.then_inc(agg_done, 1)

            def step(s, b):
                if live(s, s):
                    pe.wait_ge(agg_copied, s + 1)
                    for c in range(C):
                        if not isinstance(s, int) or s >= 1:
                            pe.wait_ge(normed_ready, C * (s - 1) + c + 1)
                        pe.matmul(ps_h[:, c, :], w1g[:, c * P:(c + 1) * P], agg[:],
                                  start=True, stop=True).then_inc(h_done, 1)
                if live(s - 2, s):
                    pe.wait_ge(chosen_ready, s - 1)
                    ch = chosen[:, b, :]
                    W = JT * KE
                    pe.matmul(ps_d[:, PR:PR + W], before[:], ch, start=True, stop=False)
                    for d in range(1, JT):
                        pe.matmul(ps_d[:, PR + d * KE:PR + W], ones_bf[:], ch[:, 0:W - d * KE],
                                  start=False, stop=(d == JT - 1))
                    for j in range(JT):
                        mm = pe.matmul(ps_d[:, TO:TO + KE], ones_bf[:], ch[:, j * KE:(j + 1) * KE],
                                       start=(j == 0), stop=(j == JT - 1))
                    mm.then_inc(prefix_done, 1)
                if live(s - 1, s):
                    if not isinstance(s, int) or s >= 2:
                        pe.wait_ge(gnn_copied, s - 1)
                    for c in range(C):
                        pe.wait_ge(hidden_ready, C * (s - 1) + c + 1)
                        mm = pe.matmul(ps_a[:], w2g[:, c, :], hidden[:, c, :],
                                       start=(c == 0), stop=(c == C - 1))
                    mm.then_inc(gnn_done, 1)
                if live(s, s):
                    pe.wait_ge(sq_sum_ready, s + 1)
                    if not isinstance(s, int) or s >= 2:
                        pe.wait_ge(prefix_read, s - 1)
                    for j in range(JT):
                        mm = pe.matmul(ps_d[:, MS + j:MS + j + 1], sq_sum[:, j * P:(j + 1) * P],
                                       ones[:, 0:1], start=True, stop=True)
                    mm.then_inc(ms_done, 1)
                if live(s - 1, s):
                    pe.wait_ge(gnn_copied, s)
                    if not isinstance(s, int) or s + 1 <= G:
                        pe.wait_ge(agg_copied, min(s + 1, G) if isinstance(s, int) else s + 1)
                    for j in range(JT):
                        mm = pe.transpose(ps_b[:, j * P:(j + 1) * P], gnn_t[:, j * P:(j + 1) * P], ident[:])
                    mm.then_inc(gnn_turned, 1)
                if live(s, s):
                    pe.wait_ge(diag_ready, s + 1)
                    if not isinstance(s, int) or s >= 2:
                        pe.wait_ge(xn2_copied, s - 1)
                    pe.matmul(ps_c[:], ones[:], rrms_diag[:].rearrange("p j n -> p (j n)"),
                              start=True, stop=True).then_inc(spread_done, 1)
                if live(s + 1, s):
                    aggregate(s + 1, 1 - b)
                if live(s - 1, s):
                    pe.wait_ge(xn2_ready, s)
                    pe.wait_ge(spread_copied, min(s + 1, G) if isinstance(s, int) else s + 1)
                    for j in range(JT):
                        mm = pe.transpose(ps_c[:, j * P:(j + 1) * P], payload[:, 1 - b, j, 0:P], ident[:])
                    mm.then_inc(xn2_turned, 1)
                    pe.wait_ge(xn2_copied, s)
                    pe.wait_ge(ms_ready, min(s + 1, G) if isinstance(s, int) else s + 1)
                    for j in range(JT):
                        mm = pe.matmul(ps_d[:, LG + j * E:LG + (j + 1) * E], xn2_t[:, j * P:(j + 1) * P],
                                       wg[:], start=True, stop=True)
                    mm.then_inc(logits_done, 1)

            pe.wait_ge(dve_consts, 3)
            aggregate(0, 0)
            steps(pe, step)

            def turn(i, b, first):
                pe.wait_ge(slots_loaded[b], 8 * (i - b) + 16)
                if not first:
                    pe.wait_ge(slots_copied, i - 1)
                for h in range(HT):
                    mm = pe.transpose((ps_a, ps_d)[b][:, h * P:(h + 1) * P],
                                      slot_rows[:, b, h, 0:P], ident[:])
                mm.then_inc(slots_turned, 1)

            def layer1(i, b):
                pe.wait_ge(slots_copied, i + 1)
                pe.wait_ge(block_ready, i + 1)
                for c in range(C):
                    mm = pe.matmul(ps_h[:, 2 * b + c // 2, (c % 2) * SLOTS:(c % 2 + 1) * SLOTS],
                                   block_w[:, b, c * P:(c + 1) * P], slot_t[:, b, :],
                                   start=True, stop=True)
                    if c % 2:
                        mm.then_inc(fh_done, 1)

            def layer2(i, b, first):
                y = (ps_b, ps_c)[b]
                pe.wait_ge(gelu_ready, C * i + C)
                if not first:
                    pe.wait_ge(y_chain, i - 1)
                for h in range(HT):
                    for c in range(C):
                        mm = pe.matmul(y[:, h * P:(h + 1) * P], gelu_t[:, b, c, h * P:(h + 1) * P],
                                       block_w[:, b, H + c * P:H + (c + 1) * P],
                                       start=(c == 0), stop=(c == C - 1))
                mm.then_inc(y_done, 1)

            turn(0, 0, True)
            layer1(0, 0)
            turn(1, 1, True)
            layer1(1, 1)
            layer2(0, 0, True)
            turn(2, 0, False)
            layer1(2, 0)
            layer2(1, 1, True)
            turn(3, 1, False)
            with pe.Fori(0, NT // 2 - 2) as pair:
                for d, b in ((3, 1), (4, 0)):
                    layer1(pair * 2 + d, b)
                    layer2(pair * 2 + (d - 1), 1 - b, False)
                    turn(pair * 2 + (d + 1), 1 - b, False)
            layer1(NT - 1, 1)
            layer2(NT - 2, 0, False)
            layer2(NT - 1, 1, False)

        @block.scalar
        def _(act):
            def copy_agg(t):
                act.wait_ge(agg_done, t + 1)
                if not isinstance(t, int) or t >= 1:
                    act.wait_ge(h_done, C * t)
                act.copy(agg[:], ps_b[:]).then_inc(agg_copied, 1)

            def step(s, b):
                if live(s, s):
                    if not isinstance(s, int) or s >= 1:
                        act.wait_ge(sq_sum_ready, s)
                    for c in range(C):
                        act.wait_ge(h_done, C * s + c + 1)
                        act.activation(squares[:, c, :], ps_h[:, c, :], ACT.Square,
                                       bias=vec_cols[:, GB1 + c:GB1 + c + 1]).then_inc(squares_ready, 1)
                if live(s - 1, s):
                    act.wait_ge(gnn_done, s)
                    if not isinstance(s, int) or s >= 2:
                        act.wait_ge(gnn_turned, s - 1)
                    act.activation(gnn_t[:], ps_a[:], ACT.Identity,
                                   bias=vec_cols[:, GB2:GB2 + 1]).then_inc(gnn_copied, 1)
                if live(s, s):
                    act.wait_ge(spread_done, s + 1)
                    if not isinstance(s, int) or s >= 1:
                        act.wait_ge(normed_ready, C * s)
                    act.copy(rrms_all[:], ps_c[:]).then_inc(spread_copied, 1)
                if live(s + 1, s):
                    copy_agg(s + 1)
                if live(s - 1, s):
                    act.wait_ge(xn2_turned, s)
                    if not isinstance(s, int) or s >= 2:
                        act.wait_ge(logits_done, s - 1)
                    act.copy(xn2_t[:], ps_c[:]).then_inc(xn2_copied, 1)
                if live(s, s):
                    if not isinstance(s, int) or s >= 1:
                        act.wait_ge(gnn_done, s)
                    for c in range(C):
                        act.wait_ge(normed_ready, C * s + c + 1)
                        act.activation(hidden[:, c, :], normed[:, c, :], ACT.Silu,
                                       scale=vec_cols[:, GRW + c:GRW + c + 1]).then_inc(hidden_ready, 1)
                if live(s - 1, s):
                    act.wait_ge(gap_ready, s)
                    if not isinstance(s, int) or s >= 2:
                        act.wait_ge(rows_ready, s - 1)
                    act.activation(half_tanh[:], gap[:], ACT.Tanh, scale=0.5).then_inc(tanh_ready, 1)

            act.wait_ge(dve_consts, 3)
            copy_agg(0)
            steps(act, step)

            def copy_slots(i, b, first):
                act.wait_ge(slots_turned, i + 1)
                if not first:
                    act.wait_ge(fh_done, 2 * (i - 1))
                act.copy(slot_t[:, b, :], (ps_a, ps_d)[b][:, 0:SLOTS]).then_inc(slots_copied, 1)

            def gelu(i, b, first):
                if not first:
                    act.wait_ge(y_done, i - 1)
                for c in range(C):
                    act.wait_ge(fh_done, 2 * i + c // 2 + 1)
                    act.activation(gelu_t[:, b, c, :],
                                   ps_h[:, 2 * b + c // 2, (c % 2) * SLOTS:(c % 2 + 1) * SLOTS], ACT.Gelu,
                                   bias=block_w[:, b, OB1 + c:OB1 + c + 1]).then_inc(gelu_ready, 1)

            copy_slots(0, 0, True)
            copy_slots(1, 1, True)
            gelu(0, 0, True)
            copy_slots(2, 0, False)
            gelu(1, 1, True)
            with act.Fori(0, NT // 2 - 2) as pair:
                for d, b in ((3, 1), (4, 0)):
                    copy_slots(pair * 2 + d, b, False)
                    gelu(pair * 2 + (d - 1), 1 - b, False)
            copy_slots(NT - 1, 1, False)
            gelu(NT - 2, 0, False)
            gelu(NT - 1, 1, False)

        @block.vector
        def _(dve):
            dve.wait_ge(consts_loaded, 16 * 6)
            dve.wait_ge(pool_consts, 4)
            dve.wait_ge(vecs_turned, 1)
            dve.tensor_copy(vec_cols[:], ps_d[:, 0:NV]).then_inc(dve_consts, 1)
            dve.tensor_scalar(eps_ident[:], ident[:], eps_col[:, 0:1], None, ALU.mult).then_inc(dve_consts, 1)
            for k in range(TOP_K):
                dve.tensor_scalar(region_base[:, k * E:(k + 1) * E], expert_no[:], float(REGION),
                                  float(k * E * REGION), ALU.mult, ALU.add)
                m = dve.tensor_scalar(next_row[:, k * E:(k + 1) * E], expert_no[:], float(REGION),
                                      float(k * E * REGION), ALU.mult, ALU.add)
            m.then_inc(dve_consts, 1)

            def layer_norm_stats(source, stats, mv, var, chain):
                for j in range(JT):
                    m = dve.bn_stats(stats[:, j, :], source(j))
                chain.link(m, wait_apart)
                for j in range(JT):
                    m = dve.bn_aggr(mv[:, j, :], stats[:, j, :])
                chain.link(m)
                return dve.tensor_scalar(var[:], mv[:, :, 1], LN_EPS, None, ALU.add)

            def ln1_stats(t, b):
                wait_apart(dve, x_loaded[b], 8 * (t - b) + 16)
                if not isinstance(t, int) or t >= 1:
                    dve.wait_ge(rstd1_ready, t)
                layer_norm_stats(lambda j: xs[:, bass.ds(t * JT + j, 1), :].rearrange("p a d -> p (a d)"),
                                 stats1, mv1, var1, Chain(dve, ln1_chain, t * 2)).then_inc(var1_ready, 1)

            def ln1_apply(t, b):
                dve.wait_ge(rstd1_ready, t + 1)
                if not isinstance(t, int) or t >= 2:
                    dve.wait_ge(agg_done, t - 1)
                for j in range(JT):
                    m = dve.tensor_scalar(xn[:, b, j, :],
                                          xs[:, bass.ds(t * JT + j, 1), :].rearrange("p a d -> p (a d)"),
                                          mv1[:, j, 0:1], rstd1[:, j:j + 1], ALU.subtract, ALU.mult)
                m.then_inc(xn_ready, 1)

            def gate(t, b):
                chain = Chain(dve, gate_chain, t * 4)
                dve.wait_ge(logits_done, t + 1)
                chain.link(dve.tensor_tensor(
                    logits[:], ps_d[:, LG:LG + JT * E].rearrange("p (j e) -> p j e", j=JT),
                    bg_all[:].rearrange("p (a e) -> p a e", a=1).to_broadcast([P, JT, E]), ALU.add), wait_apart)
                for j in range(JT):
                    m = dve.max(top_vals[:, j, :], logits[:, j, :])
                chain.link(m, wait_apart)
                for j in range(JT):
                    m = dve.max_index(top_idx[:, j, :], top_vals[:, j, :], logits[:, j, :])
                if not isinstance(t, int) or t >= 1:
                    dve.wait_ge(tanh_ready, t)
                dve.tensor_tensor(gap[:], top_vals[:, :, 0], top_vals[:, :, 1],
                                  ALU.subtract).then_inc(gap_ready, 1)
                chain.link(m)
                chain.link(dve.tensor_copy(top_no[:], top_idx[:, :, 0:TOP_K]))
                if not isinstance(t, int) or t >= 2:
                    dve.wait_ge(prefix_done, t - 1)
                for k in range(TOP_K):
                    m = dve.tensor_tensor(
                        chosen[:, b, :].rearrange("p (j k e) -> p j k e", j=JT, k=TOP_K)[:, :, k, :],
                        top_no[:, :, k:k + 1].to_broadcast([P, JT, E]),
                        expert_no[:].rearrange("p (a e) -> p a e", a=1).to_broadcast([P, JT, E]),
                        ALU.is_equal)
                m.then_inc(chosen_ready, 1)

            def place(t, b):
                chain = Chain(dve, row_chain, t * 4)
                dve.wait_ge(prefix_done, t + 1)
                chain.link(dve.tensor_tensor(
                    row_cand[:], ps_d[:, PR:PR + JT * KE].rearrange("p (j g) -> p j g", j=JT),
                    next_row[:].rearrange("p (a g) -> p a g", a=1).to_broadcast([P, JT, KE]), ALU.add))
                dve.tensor_tensor(next_row[:], next_row[:], ps_d[:, TO:TO + KE],
                                  ALU.add).then_inc(prefix_read, 1)
                chain.link(dve.tensor_tensor(
                    row_cand[:], row_cand[:], chosen[:, b, :].rearrange("p (j g) -> p j g", j=JT), ALU.mult))
                chain.link(dve.tensor_reduce(
                    row_f[:], row_cand[:].rearrange("p j (k e) -> p (j k) e", k=TOP_K), AX.X, ALU.add))
                dve.wait_ge(tanh_ready, t + 1)
                for k in range(TOP_K):
                    dve.tensor_scalar(payload[:, b, :, WEIGHT + k], half_tanh[:], 0.5 - k, 0.5,
                                      ALU.mult, ALU.add)
                dve.tensor_copy(payload[:, b, :, TOKEN].bitcast(I32), token_no[:])
                chain.link(dve.tensor_copy(row_idx[:, b, :], row_f[:]))
                dve.tensor_scalar(token_no[:], token_no[:], float(GROUP), None, ALU.add).then_inc(rows_ready, 1)

            def step(s, b):
                if live(s - 2, s):
                    place(s - 2, b)
                if live(s, s):
                    dve.wait_ge(squares_ready, C * s + C)
                    chain = Chain(dve, sq_chain, s * 1)
                    chain.link(dve.tensor_tensor(sq_pair[:], squares[:, 0:2, :], squares[:, 2:4, :], ALU.add))
                    if not isinstance(s, int) or s >= 1:
                        dve.wait_ge(ms_done, s)
                    dve.tensor_tensor(sq_sum[:], sq_pair[:, 0, :], sq_pair[:, 1, :],
                                      ALU.add).then_inc(sq_sum_ready, 1)
                if live(s - 1, s):
                    dve.wait_ge(gnn_turned, s)
                    x2 = xs[:, bass.ds((s - 1) * JT, JT), :]
                    dve.tensor_tensor(x2, x2, ps_b[:].rearrange("p (j d) -> p j d", j=JT),
                                      ALU.add).then_inc(x2_ready, 1)
                if live(s, s):
                    dve.wait_ge(ms_done, s + 1)
                    if not isinstance(s, int) or s >= 1:
                        dve.wait_ge(rrms_ready, s)
                    dve.tensor_scalar(mean_sq[:], ps_d[:, MS:MS + JT], 1.0 / H, RMS_EPS,
                                      ALU.mult, ALU.add).then_inc(ms_ready, 1)
                if live(s - 1, s):
                    wait_apart(dve, x2_ready, s)
                    if not isinstance(s, int) or s >= 2:
                        dve.wait_ge(rstd2_ready, s - 1)
                    layer_norm_stats(
                        lambda j: xs[:, bass.ds((s - 1) * JT + j, 1), :].rearrange("p a d -> p (a d)"),
                        stats2, mv2, var2, Chain(dve, ln2_chain, (s - 1) * 2)).then_inc(var2_ready, 1)
                if live(s, s):
                    dve.wait_ge(rrms_ready, s + 1)
                    if not isinstance(s, int) or s >= 1:
                        dve.wait_ge(spread_done, s)
                    dve.tensor_tensor(
                        rrms_diag[:], ident[:].rearrange("p (a n) -> p a n", a=1).to_broadcast([P, JT, P]),
                        rrms[:].rearrange("p (j a) -> p j a", a=1).to_broadcast([P, JT, P]),
                        ALU.mult).then_inc(diag_ready, 1)
                if live(s + 2, s):
                    ln1_stats(s + 2, b)
                if live(s - 1, s):
                    dve.wait_ge(rstd2_ready, s)
                    if not isinstance(s, int) or s >= 3:
                        dve.wait_ge(dispatched[1 - b], (s - 2 + b) * (8 * JT * TOP_K) if not isinstance(s, int)
                                    else 16 * JT * TOP_K * ((s - 2 + b) // 2))
                    for j in range(JT):
                        m = dve.tensor_scalar(payload[:, 1 - b, j, 0:P],
                                              xs[:, bass.ds((s - 1) * JT + j, 1), :].rearrange("p a d -> p (a d)"),
                                              mv2[:, j, 0:1], rstd2[:, j:j + 1], ALU.subtract, ALU.mult)
                    m.then_inc(xn2_ready, 1)
                if live(s, s):
                    dve.wait_ge(spread_copied, s + 1)
                    if not isinstance(s, int) or s >= 1:
                        dve.wait_ge(hidden_ready, C * s)
                    for c in range(C):
                        dve.scalar_tensor_tensor(normed[:, c, :], ps_h[:, c, :],
                                                 vec_cols[:, GB1 + c:GB1 + c + 1], rrms_all[:],
                                                 ALU.add, ALU.mult).then_inc(normed_ready, 1)
                if live(s + 2, s):
                    ln1_apply(s + 2, b)
                if live(s - 1, s):
                    gate(s - 1, 1 - b)

            dve.wait_ge(dve_consts, 3)
            ln1_stats(0, 0)
            ln1_apply(0, 0)
            ln1_stats(1, 1)
            ln1_apply(1, 1)
            steps(dve, step)

            chain = Chain(dve, table_chain, 0)
            dve.wait_ge(rows_ready, G)
            chain.link(dve.tensor_copy(region_end[:], next_row[:]))
            dve.memset(zeros_e[:], 0.0).then_inc(ends_ready, 1)
            chain.link(dve.tensor_tensor(tiles_f[:], next_row[:], region_base[:], ALU.subtract))
            chain.link(dve.tensor_scalar(count_i[:], tiles_f[:], float(SLOTS - 1), None, ALU.add))
            chain.link(dve.tensor_scalar(tiles_i[:], count_i[:], SLOTS.bit_length() - 1, None,
                                         ALU.logical_shift_right))
            chain.link(dve.tensor_copy(tiles_f[:], tiles_i[:]))
            dve.tensor_scalar(skip[:], tiles_f[:], -float(SLOTS), float(REGION), ALU.mult, ALU.add)
            for k in range(TOP_K):
                m = dve.tensor_tensor_scan(tiles_cum[:, k * E:(k + 1) * E], tiles_f[:, k * E:(k + 1) * E],
                                           zeros_e[:], 0.0, ALU.add, ALU.add)
            chain.link(m)
            for k in range(TOP_K):
                ks = slice(k * E, (k + 1) * E)
                tab = slice(k * TILES, (k + 1) * TILES)
                chain.link(dve.tensor_tensor(
                    passed[:], tiles_cum[:, ks].rearrange("p (a e) -> p a e", a=1).to_broadcast([P, TILES, E]),
                    tile_no[:].rearrange("p (i a) -> p i a", a=1).to_broadcast([P, TILES, E]), ALU.is_le))
                dve.tensor_reduce(tile_expert[:], passed[:], AX.X, ALU.add)
                chain.link(dve.tensor_tensor(
                    skipped[:], passed[:],
                    skip[:, ks].rearrange("p (a e) -> p a e", a=1).to_broadcast([P, TILES, E]), ALU.mult))
                chain.link(dve.tensor_reduce(tile_row[:], skipped[:], AX.X, ALU.add))
                chain.link(dve.scalar_tensor_tensor(tile_row[:], tile_no[:], float(SLOTS), tile_row[:],
                                                    ALU.mult, ALU.add))
                chain.link(dve.tensor_scalar(over[:], tile_expert[:], float(E), float(DUMMY),
                                             ALU.is_ge, ALU.mult))
                chain.link(dve.scalar_tensor_tensor(tile_row[:], tile_row[:], float(k * E * REGION), over[:],
                                                    ALU.add, ALU.add))
                dve.tensor_scalar(expert_tab[:, tab], tile_expert[:], float(E - 1), float(BLOCK), ALU.min, ALU.mult)
                chain.link(dve.tensor_scalar(row_tab[:, tab], tile_row[:], float(DUMMY), None, ALU.min))
            dve.wait_ge(experts_loaded, 16 * 3 * E)
            dve.tensor_copy(experts[:].rearrange("p (e w) -> p e w", e=E)[:, :, OB1:OB1 + C],
                            vec_cols[:, FB1:FB1 + E * C].rearrange("p (e c) -> p e c", e=E)
                            ).then_inc(tables_ready, 1)
            dve.wait_ge(tables_ready, 1)

            def copy_block(i, b, first):
                if not first:
                    dve.wait_ge(y_done, i - 1)
                at = dve.value_load(expert_tab[0:1, bass.ds(i, 1)], min_val=0, max_val=(E - 1) * BLOCK)
                dve.tensor_copy(block_w[:, b, :], experts[:, bass.ds(at, BLOCK)]).then_inc(block_ready, 1)

            def finish(i, b, k, first):
                y = (ps_b, ps_c)[b]
                dve.wait_ge(y_done, i + 1)
                dve.tensor_tensor(
                    y_bias[:, b, :, :], y[:, 0:SLOTS].rearrange("p (h d) -> p h d", h=HT),
                    block_w[:, b, OB2:OB2 + P].rearrange("p (a d) -> p a d", a=1).to_broadcast([P, HT, P]),
                    ALU.add).then_inc(y_chain, 1)
                dve.wait_ge(y_chain, i + 1)
                if not first:
                    dve.wait_ge(added[b], (i - b) * (8 * HT))
                dve.tensor_tensor(y_out[:, b, :, :], y_bias[:, b, :, :],
                                  slot_rows[:, b, :, WEIGHT + k:WEIGHT + k + 1].to_broadcast([P, HT, P]),
                                  ALU.mult).then_inc(y_ready, 1)

            copy_block(0, 0, True)
            copy_block(1, 1, True)
            finish(0, 0, 0, True)
            copy_block(2, 0, False)
            finish(1, 1, 0, True)
            with dve.Fori(0, (TILES - 3) // 2) as pair:
                for d, b in ((3, 1), (4, 0)):
                    copy_block(pair * 2 + d, b, False)
                    finish(pair * 2 + (d - 1), 1 - b, 0, False)
            copy_block(TILES, 1, False)
            finish(TILES - 1, 0, 0, False)
            with dve.Fori(0, TILES // 2) as pair:
                for d, b in ((TILES + 1, 0), (TILES + 2, 1)):
                    copy_block(pair * 2 + d, b, False)
                    finish(pair * 2 + (d - 1), 1 - b, 1, False)
            finish(NT - 1, 1, 1, False)


_IN = ["x", "adj_t", "epsilon", "g_w1", "vectors", "g_w2", "f_wg", "f_bg", "f_w1", "f_w2", "f_b2"]


def kernel(x, adj, L0_gnn_epsilon, L0_gnn_W1, L0_gnn_b1, L0_gnn_rms_weight, L0_gnn_W2, L0_gnn_b2,
           L0_ffn_Wg, L0_ffn_bg, L0_ffn_W1, L0_ffn_b1, L0_ffn_W2, L0_ffn_b2):
    import concourse.bacc as bacc
    from concourse.bass_utils import run_bass_kernel_spmd

    B, N, D = x.shape
    E = L0_ffn_Wg.shape[1]
    given = {
        "x": np.asarray(x).reshape(B * N, D),
        "adj_t": np.asarray(adj).transpose(0, 2, 1),
        "epsilon": np.asarray(L0_gnn_epsilon).reshape(1, 1),
        "g_w1": L0_gnn_W1,
        "vectors": np.concatenate([np.asarray(a).reshape(-1, D) for a in
                                   (L0_gnn_b1, L0_gnn_rms_weight, L0_gnn_b2, L0_ffn_b1)]),
        "g_w2": L0_gnn_W2,
        "f_wg": L0_ffn_Wg,
        "f_bg": np.asarray(L0_ffn_bg).reshape(1, E),
        "f_w1": L0_ffn_W1,
        "f_w2": L0_ffn_W2,
        "f_b2": L0_ffn_b2,
    }
    nc = bacc.Bacc("TRN2", target_bir_lowering=False, num_devices=1)
    arrays, args = {}, []
    for name in _IN:
        a = np.ascontiguousarray(given[name])
        arrays[f"in_{name}"] = a
        args.append(nc.dram_tensor(f"in_{name}", a.shape, mybir.dt.from_np(a.dtype), kind="ExternalInput").ap())
    out = nc.dram_tensor("out_y", (B * N, D), F32, kind="ExternalOutput").ap()
    moe_gnn(nc, *args, out)
    r = run_bass_kernel_spmd(nc, [arrays], core_ids=[0])
    return r.results[0]["out_y"].reshape(B, N, D)
```

```python
from contextlib import ExitStack

import numpy as np

import concourse.bass as bass
from concourse import mybir

F32 = mybir.dt.float32
BF16 = mybir.dt.bfloat16
I32 = mybir.dt.int32
U32 = mybir.dt.uint32
ALU = mybir.AluOpType
ACT = mybir.ActivationFunctionType
AX = mybir.AxisListType

P = 128
JT = 4
GROUP = JT * P
SLOTS = 256
HT = SLOTS // P
TOP_K = 2
RING = 8
BLOCKS = 4
LN_EPS = 1e-5
RMS_EPS = 1e-6

TOKEN, WEIGHT, ROW = P, P + 1, P + 3


class Chain:

    def __init__(self, engine, sem, done):
        self.engine, self.sem, self.done, self.n = engine, sem, done, 0

    def link(self, instruction, wait=None):
        self.n += 1
        instruction.then_inc(self.sem, 1)
        if wait:
            wait(self.engine, self.sem, self.done + self.n)
        else:
            self.engine.wait_ge(self.sem, self.done + self.n)


def moe_gnn(nc, x, adj_t, epsilon, g_w1, vectors, g_w2, f_wg, f_bg, f_w1, f_w2, f_b2, out):
    T, D = x.shape
    H = g_w1.shape[1]
    E = f_wg.shape[1]
    NODES = adj_t.shape[1]
    C = H // P
    G = T // GROUP
    BPT = P // NODES
    KE = TOP_K * E
    REGION = T + SLOTS
    DUMMY = KE * REGION
    TILES = (T + E * (SLOTS - 1)) // SLOTS
    NT = TOP_K * TILES
    BLOCK = 2 * C * P + C + P
    OB1, OB2 = 2 * C * P, 2 * C * P + C
    NV = vectors.shape[0]
    GB1, GRW, GB2, FB1 = 0, C, 2 * C, 2 * C + 1
    assert D == P and C == 4 and BPT == 2 and G % 2 == 0 and TILES % 2 == 1 and HT == 2

    with ExitStack() as ctx:
        def sb(name, shape, dt=F32):
            return ctx.enter_context(nc.sbuf_tensor(name, shape, dt))

        def sem(name):
            return ctx.enter_context(nc.semaphore(name))

        rows = nc.dram_tensor("dispatched_rows", (DUMMY + SLOTS, ROW), F32).ap()

        ident = sb("ident", [P, P])
        eps_ident = sb("eps_ident", [P, P])
        ones = sb("ones", [P, P])
        ones_bf = sb("ones_bf", [P, P], BF16)
        before = sb("before", [P, P], BF16)
        neg_half = sb("neg_half", [P, JT])
        expert_no = sb("expert_no", [P, E])
        tile_no = sb("tile_no", [P, TILES])
        region_base = sb("region_base", [P, KE])
        token_no = sb("token_no", [P, JT], I32)
        pad_rows = sb("pad_rows", [P, HT, ROW])
        eps_col = sb("eps_col", [P, 1])
        bg_all = sb("bg_all", [P, E])
        w1g = sb("w1g", [P, H])
        w2g = sb("w2g", [P, C, P])
        wg = sb("wg", [P, E])
        vec_rows = sb("vec_rows", [NV, P])
        vec_cols = sb("vec_cols", [P, NV])
        experts = sb("experts", [P, E * BLOCK])

        xs = sb("xs", [P, G * JT, P])
        adj_blocks = sb("adj_blocks", [P, 2, JT, P])
        stats1 = sb("stats1", [P, JT, 6])
        stats2 = sb("stats2", [P, JT, 6])
        mv1 = sb("mv1", [P, JT, 2])
        mv2 = sb("mv2", [P, JT, 2])
        var1 = sb("var1", [P, JT])
        var2 = sb("var2", [P, JT])
        rstd1 = sb("rstd1", [P, JT])
        rstd2 = sb("rstd2", [P, JT])
        xn = sb("xn", [P, 2, JT, P])
        agg = sb("agg", [P, 2, GROUP])
        h_bias = sb("h_bias", [P, 2, C, GROUP])
        squares = sb("squares", [P, C, GROUP])
        sq_pair = sb("sq_pair", [P, 2, GROUP])
        sq_sum = sb("sq_sum", [P, GROUP])
        mean_sq = sb("mean_sq", [P, JT])
        rrms = sb("rrms", [P, JT])
        rrms_diag = sb("rrms_diag", [P, JT, P])
        rrms_all = sb("rrms_all", [P, GROUP])
        normed = sb("normed", [P, C, GROUP])
        hidden = sb("hidden", [P, C, GROUP])
        gnn_t = sb("gnn_t", [P, GROUP])
        payload = sb("payload", [P, 2, JT, ROW])
        xn2_t = sb("xn2_t", [P, GROUP])
        logits = sb("logits", [P, JT, E])
        top_vals = sb("top_vals", [P, JT, 8])
        top_idx = sb("top_idx", [P, JT, 8], U32)
        top_no = sb("top_no", [P, JT, TOP_K])
        gap = sb("gap", [P, JT])
        half_tanh = sb("half_tanh", [P, JT])
        chosen = sb("chosen", [P, 2, JT * KE], BF16)
        next_row = sb("next_row", [P, KE])
        row_cand = sb("row_cand", [P, JT, KE])
        row_f = sb("row_f", [P, JT * TOP_K])
        row_idx = sb("row_idx", [P, 2, JT * TOP_K], I32)

        region_end = sb("region_end", [P, KE], I32)
        count_i = sb("count_i", [P, KE], I32)
        tiles_i = sb("tiles_i", [P, KE], I32)
        tiles_f = sb("tiles_f", [P, KE])
        zeros_e = sb("zeros_e", [P, E])
        tiles_cum = sb("tiles_cum", [P, KE])
        skip = sb("skip", [P, KE])
        passed = sb("passed", [P, TILES, E])
        skipped = sb("skipped", [P, TILES, E])
        tile_expert = sb("tile_expert", [P, TILES])
        tile_row = sb("tile_row", [P, TILES])
        over = sb("over", [P, TILES])
        expert_tab = sb("expert_tab", [P, NT], I32)
        row_tab = sb("row_tab", [P, NT], I32)

        slot_rows = sb("slot_rows", [P, RING, HT, ROW])
        slot_t = sb("slot_t", [P, 2, SLOTS])
        block_w = sb("block_w", [P, BLOCKS, BLOCK])
        gelu_t = sb("gelu_t", [P, 2, C, SLOTS])
        y_bias = sb("y_bias", [P, RING, HT, P])
        y_out = sb("y_out", [P, RING, HT, P])

        ps_h = ctx.enter_context(nc.psum_tensor("ps_h", [P, C, 512], F32))
        ps_a = ctx.enter_context(nc.psum_tensor("ps_a", [P, 512], F32))
        ps_b = ctx.enter_context(nc.psum_tensor("ps_b", [P, 512], F32))
        ps_c = ctx.enter_context(nc.psum_tensor("ps_c", [P, 512], F32))
        ps_d = ctx.enter_context(nc.psum_tensor("ps_d", [P, 512], F32))
        MS, LG, PR, TO = 0, 8, 64, 192

        consts_loaded = sem("consts_loaded")
        experts_loaded = sem("experts_loaded")
        pool_consts = sem("pool_consts")
        dve_consts = sem("dve_consts")
        vecs_turned = sem("vecs_turned")
        x_loaded = [sem(f"x_loaded{b}") for b in range(2)]
        adj_loaded = [sem(f"adj_loaded{b}") for b in range(2)]
        ln1_chain = sem("ln1_chain")
        var1_ready = sem("var1_ready")
        rstd1_ready = sem("rstd1_ready")
        xn_ready = sem("xn_ready")
        agg_done = sem("agg_done")
        agg_copied = sem("agg_copied")
        h_done = sem("h_done")
        h_copied = sem("h_copied")
        squares_ready = sem("squares_ready")
        sq_chain = sem("sq_chain")
        sq_sum_ready = sem("sq_sum_ready")
        ms_done = sem("ms_done")
        ms_ready = sem("ms_ready")
        rrms_ready = sem("rrms_ready")
        diag_ready = sem("diag_ready")
        spread_done = sem("spread_done")
        spread_copied = sem("spread_copied")
        normed_ready = sem("normed_ready")
        hidden_ready = sem("hidden_ready")
        gnn_done = sem("gnn_done")
        gnn_copied = sem("gnn_copied")
        gnn_turned = sem("gnn_turned")
        x2_ready = sem("x2_ready")
        x2_stored = sem("x2_stored")
        ln2_chain = sem("ln2_chain")
        var2_ready = sem("var2_ready")
        rstd2_ready = sem("rstd2_ready")
        xn2_ready = sem("xn2_ready")
        xn2_turned = sem("xn2_turned")
        xn2_copied = sem("xn2_copied")
        logits_done = sem("logits_done")
        gate_chain = sem("gate_chain")
        gap_ready = sem("gap_ready")
        tanh_ready = sem("tanh_ready")
        chosen_ready = sem("chosen_ready")
        prefix_done = sem("prefix_done")
        prefix_read = sem("prefix_read")
        row_chain = sem("row_chain")
        rows_ready = sem("rows_ready")
        dispatched = [sem(f"dispatched{b}") for b in range(2)]
        table_chain = sem("table_chain")
        ends_ready = sem("ends_ready")
        padded = sem("padded")
        tables_ready = sem("tables_ready")
        slots_loaded = [sem(f"slots_loaded{r}") for r in range(RING)]
        slots_turned = sem("slots_turned")
        slots_copied = sem("slots_copied")
        block_ready = sem("block_ready")
        fh_done = sem("fh_done")
        gelu_ready = sem("gelu_ready")
        y_done = sem("y_done")
        y_chain = sem("y_chain")
        y_ready = sem("y_ready")
        added = [sem(f"added{r}") for r in range(RING)]

        def wait_apart(engine, semaphore, value):
            if not isinstance(value, int):
                value = engine.to_reg(value)
                engine.wait_ge(pool_consts, 1)
            engine.wait_ge(semaphore, value)

        def live(t):
            return not isinstance(t, int) or 0 <= t < G

        def steps(engine, step):
            for s in range(-3, 4):
                step(s, s % 2)
            with engine.Fori(2, G // 2 - 2) as pair:
                step(pair * 2, 0)
                step(pair * 2 + 1, 1)
            for s in range(G - 4, G + 2):
                step(s, s % 2)

        def after(engine, semaphore, value):
            if not isinstance(value, int) or value >= 1:
                engine.wait_ge(semaphore, value)

        def tiles(engine, first, last, tile):
            start = first + (last - first) % RING
            while start < min(RING + 1, last):
                start = min(start + RING, last)
            for i in range(first, start):
                tile(i, i % RING)
            if last > start:
                with engine.Fori(0, (last - start) // RING) as turn_no:
                    for d in range(RING):
                        tile(turn_no * RING + (start + d), (start + d) % RING)

        x_view = x.rearrange("(r p) d -> p r d", p=P)
        out_view = out.rearrange("(r p) d -> p r d", p=P)
        adj_view = adj_t.rearrange("(r h) m n -> h m r n", h=BPT)

        block = ctx.enter_context(nc.Block())

        @block.sync
        def _(sp):
            for dst, src in (
                (w1g[:], g_w1), (w2g[:], g_w2.rearrange("(c p) d -> p c d", p=P)),
                (wg[:], f_wg), (vec_rows[:], vectors),
                (eps_col[:], epsilon.to_broadcast([P, 1])), (bg_all[:], f_bg.to_broadcast([P, E])),
            ):
                sp.dma_start(dst, src).then_inc(consts_loaded, 16)

            def load_x(t, b):
                after(sp, x_loaded[b], 8 * (t - b))
                sp.dma_start(xs[:, bass.ds(t * JT, JT), :],
                             x_view[:, bass.ds(t * JT, JT), :]).then_inc(x_loaded[b], 16)

            def load_adj(t, b):
                for h in range(BPT):
                    half = slice(h * NODES, (h + 1) * NODES)
                    sp.dma_start(adj_blocks[half, b, :, half],
                                 adj_view[h, :, bass.ds(t * JT, JT), :]).then_inc(adj_loaded[b], 16)

            load_x(0, 0)
            load_x(1, 1)
            sp.wait_ge(pool_consts, 1)
            load_adj(0, 0)
            load_adj(1, 1)
            load_x(2, 0)
            load_x(3, 1)
            for e in range(E):
                blk = experts[:, e * BLOCK:(e + 1) * BLOCK]
                sp.dma_start(blk[:, 0:H], f_w1[e]).then_inc(experts_loaded, 16)
                sp.dma_start(blk[:, H:2 * H].rearrange("p (c d) -> p c d", c=C),
                             f_w2[e].rearrange("(c p) d -> p c d", p=P)).then_inc(experts_loaded, 16)
                sp.dma_start(blk[:, OB2:OB2 + P],
                             f_b2[e:e + 1, :].to_broadcast([P, P])).then_inc(experts_loaded, 16)

            def step(s, b):
                if live(s + 4) and (not isinstance(s, int) or s >= 0):
                    load_x(s + 4, b)
                if live(s + 4) and (not isinstance(s, int) or s >= -2):
                    sp.wait_ge(agg_done, s + 3)
                    load_adj(s + 4, b)
                if live(s - 1):
                    sp.wait_ge(x2_ready, s)
                    sp.dma_start(out_view[:, bass.ds((s - 1) * JT, JT), :],
                                 xs[:, bass.ds((s - 1) * JT, JT), :]).then_inc(x2_stored, 16)

            steps(sp, step)

            sp.wait_ge(pool_consts, 3)
            sp.dma_start(rows[DUMMY:DUMMY + SLOTS, :].rearrange("(h p) c -> p h c", p=P),
                         pad_rows[:]).then_inc(padded, 16)
            sp.wait_ge(ends_ready, 1)
            for g in range(KE):
                end = sp.value_load(region_end[0:1, g:g + 1], min_val=0, max_val=DUMMY - SLOTS)
                sp.dma_start(rows[bass.ds(end, SLOTS), :].rearrange("(h p) c -> p h c", p=P),
                             pad_rows[:]).then_inc(padded, 16)

            def load_slots(i, r):
                if not isinstance(i, int) or i >= RING:
                    wait_apart(sp, added[r], 16 * HT // RING * (i - r))
                start = sp.value_load(row_tab[0:1, bass.ds(i, 1)], min_val=0, max_val=DUMMY)
                sp.dma_start(slot_rows[:, r, :, :],
                             rows[bass.ds(start, SLOTS), :].rearrange("(h p) c -> p h c", p=P)
                             ).then_inc(slots_loaded[r], 16)

            sp.wait_ge(tables_ready, 1)
            sp.wait_ge(padded, 16 * (KE + 1))
            for b in range(2):
                sp.wait_ge(dispatched[b], 16 * JT * TOP_K * (G // 2))
            tiles(sp, 0, RING, load_slots)
            tiles(sp, RING, NT, load_slots)
            sp.wait_ge(x2_stored, 16 * G)
            for r in range(RING):
                sp.wait_ge(added[r], 16 * HT * len(range(r, NT, RING)))

        @block.gpsimd
        def _(pool):
            pool.memset(adj_blocks[:], 0.0).then_inc(pool_consts, 1)
            pool.memset(ident[:], 0.0)
            pool.memset(before[:], 0.0)
            pool.memset(pad_rows[:], 0.0)
            pool.memset(neg_half[:], -0.5)
            pool.memset(ones[:], 1.0)
            pool.memset(ones_bf[:], 1.0)
            pool.iota(expert_no[:], [[1, E]], base=0, channel_multiplier=0,
                      allow_small_or_imprecise_dtypes=True)
            pool.iota(tile_no[:], [[1, TILES]], base=0, channel_multiplier=0,
                      allow_small_or_imprecise_dtypes=True)
            pool.iota(token_no[:], [[P, JT]], base=0, channel_multiplier=1)
            pool.iota(top_no[:, 0, 0:1], [[1, 1]], base=0, channel_multiplier=0,
                      allow_small_or_imprecise_dtypes=True).then_inc(pool_consts, 1)
            pool.wait_ge(pool_consts, 2)
            pool.memset(pad_rows[:, :, TOKEN:TOKEN + 1].bitcast(I32), T).then_inc(pool_consts, 1)
            pool.affine_select(out=ident[:], in_=ident[:], compare_op=ALU.not_equal, fill=1.0,
                               base=0, pattern=[[-1, P]], channel_multiplier=1)
            pool.affine_select(out=before[:], in_=before[:], compare_op=ALU.is_ge, fill=1.0,
                               base=0, pattern=[[-1, P]], channel_multiplier=1).then_inc(pool_consts, 1)

            def step(s, b):
                if live(s):
                    pool.wait_ge(ms_ready, s + 1)
                    after(pool, diag_ready, s)
                    pool.tensor_tensor(rrms[:], mean_sq[:], neg_half[:],
                                       ALU.pow).then_inc(rrms_ready, 1)
                if live(s + 3):
                    pool.wait_ge(var1_ready, s + 4)
                    after(pool, xn_ready, s + 3)
                    pool.tensor_tensor(rstd1[:], var1[:], neg_half[:],
                                       ALU.pow).then_inc(rstd1_ready, 1)
                if live(s - 1):
                    pool.wait_ge(var2_ready, s)
                    after(pool, xn2_ready, s - 1)
                    pool.tensor_tensor(rstd2[:], var2[:], neg_half[:],
                                       ALU.pow).then_inc(rstd2_ready, 1)
                if live(s - 2):
                    wait_apart(pool, rows_ready, s - 1)
                    for jk in range(JT * TOP_K):
                        pool.indirect_dma_start(
                            rows, bass.IndirectOffsetOnAxis(row_idx[:, b, jk:jk + 1], 0),
                            payload[:, b, jk // TOP_K, :], None).then_inc(dispatched[b], 16)

            steps(pool, step)

            def add_tile(i, r):
                wait_apart(pool, y_ready, i + 1)
                for h in range(HT):
                    pool.indirect_dma_start(
                        out, bass.IndirectOffsetOnAxis(slot_rows[:, r, h, TOKEN:TOKEN + 1].bitcast(I32), 0),
                        y_out[:, r, h, :], None, bounds_check=T - 1, oob_is_err=False,
                        compute_op=ALU.add).then_inc(added[r], 16)

            pool.wait_ge(x2_stored, 16 * G)
            tiles(pool, 0, TILES, add_tile)
            for r in range(RING):
                pool.wait_ge(added[r], 16 * HT * len(range(r, TILES, RING)))
            tiles(pool, TILES, NT, add_tile)

        @block.tensor
        def _(pe):
            pe.wait_ge(consts_loaded, 16 * 6)
            pe.wait_ge(pool_consts, 4)
            pe.transpose(ps_d[:, 0:NV], vec_rows[:], ident[0:NV, 0:NV]).then_inc(vecs_turned, 1)

            def step(s, b):
                if live(s - 1):
                    after(pe, x2_ready, s - 1)
                    for c in range(C):
                        pe.wait_ge(hidden_ready, C * (s - 1) + c + 1)
                        mm = pe.matmul(ps_a[:], w2g[:, c, :], hidden[:, c, :],
                                       start=(c == 0), stop=(c == C - 1))
                    mm.then_inc(gnn_done, 1)
                if live(s):
                    pe.wait_ge(sq_sum_ready, s + 1)
                    after(pe, chosen_ready, s - 1)
                    for j in range(JT):
                        mm = pe.matmul(ps_d[:, MS + j:MS + j + 1], sq_sum[:, j * P:(j + 1) * P],
                                       ones[:, 0:1], start=True, stop=True)
                    mm.then_inc(ms_done, 1)
                if live(s + 2):
                    pe.wait_ge(adj_loaded[b], 16 * (s + 2 - b) + 32)
                    pe.wait_ge(xn_ready, s + 3)
                    after(pe, agg_copied, s + 2)
                    after(pe, xn2_copied, s - 1)
                    for j in range(JT):
                        cols = ps_b[:, j * P:(j + 1) * P]
                        pe.matmul(cols, xn[:, b, j, :], adj_blocks[:, b, j, :], start=True, stop=False)
                        mm = pe.matmul(cols, xn[:, b, j, :], eps_ident[:], start=False, stop=True)
                    mm.then_inc(agg_done, 1)
                if live(s - 2):
                    pe.wait_ge(chosen_ready, s - 1)
                    pe.wait_ge(ms_ready, min(s + 1, G) if isinstance(s, int) else s + 1)
                    ch = chosen[:, b, :]
                    W = JT * KE
                    pe.matmul(ps_d[:, PR:PR + W], before[:], ch, start=True, stop=False)
                    for d in range(1, JT):
                        pe.matmul(ps_d[:, PR + d * KE:PR + W], ones_bf[:], ch[:, 0:W - d * KE],
                                  start=False, stop=(d == JT - 1))
                    for j in range(JT):
                        mm = pe.matmul(ps_d[:, TO:TO + KE], ones_bf[:], ch[:, j * KE:(j + 1) * KE],
                                       start=(j == 0), stop=(j == JT - 1))
                    mm.then_inc(prefix_done, 1)
                if live(s - 1):
                    pe.wait_ge(gnn_copied, s)
                    for j in range(JT):
                        mm = pe.transpose(ps_a[:, j * P:(j + 1) * P], gnn_t[:, j * P:(j + 1) * P], ident[:])
                    mm.then_inc(gnn_turned, 1)
                if live(s):
                    pe.wait_ge(diag_ready, s + 1)
                    after(pe, spread_copied, s)
                    pe.matmul(ps_c[:], ones[:], rrms_diag[:].rearrange("p j n -> p (j n)"),
                              start=True, stop=True).then_inc(spread_done, 1)
                if live(s + 1):
                    pe.wait_ge(agg_copied, s + 2)
                    for c in range(C):
                        after(pe, squares_ready, C * s + c + 1)
                        pe.matmul(ps_h[:, c, :], w1g[:, c * P:(c + 1) * P], agg[:, 1 - b, :],
                                  start=True, stop=True).then_inc(h_done, 1)
                if live(s - 1):
                    pe.wait_ge(xn2_ready, s)
                    pe.wait_ge(agg_copied, min(s + 3, G) if isinstance(s, int) else s + 3)
                    for j in range(JT):
                        mm = pe.transpose(ps_b[:, j * P:(j + 1) * P], payload[:, 1 - b, j, 0:P], ident[:])
                    mm.then_inc(xn2_turned, 1)
                    pe.wait_ge(xn2_copied, s)
                    pe.wait_ge(ms_ready, min(s + 1, G) if isinstance(s, int) else s + 1)
                    after(pe, prefix_read, s - 1)
                    for j in range(JT):
                        mm = pe.matmul(ps_d[:, LG + j * E:LG + (j + 1) * E], xn2_t[:, j * P:(j + 1) * P],
                                       wg[:], start=True, stop=True)
                    mm.then_inc(logits_done, 1)

            pe.wait_ge(dve_consts, 3)
            steps(pe, step)

            def turn(i, r):
                pe.wait_ge(slots_loaded[r], 16 // RING * (i - r) + 16)
                if not isinstance(i, int) or i >= 2:
                    pe.wait_ge(slots_copied, i - 1)
                for h in range(HT):
                    mm = pe.transpose((ps_a, ps_d)[r % 2][:, h * P:(h + 1) * P],
                                      slot_rows[:, r, h, 0:P], ident[:])
                mm.then_inc(slots_turned, 1)

            def layer1(i, r):
                b = r % 2
                pe.wait_ge(slots_copied, i + 1)
                pe.wait_ge(block_ready, i + 1)
                for c in range(C):
                    mm = pe.matmul(ps_h[:, 2 * b + c // 2, (c % 2) * SLOTS:(c % 2 + 1) * SLOTS],
                                   block_w[:, r % BLOCKS, c * P:(c + 1) * P], slot_t[:, b, :],
                                   start=True, stop=True)
                    if c % 2:
                        mm.then_inc(fh_done, 1)

            def layer2(i, r):
                b = r % 2
                y = (ps_b, ps_c)[b]
                pe.wait_ge(gelu_ready, C * i + C)
                if not isinstance(i, int) or i >= 2:
                    pe.wait_ge(y_chain, i - 1)
                for h in range(HT):
                    for c in range(C):
                        mm = pe.matmul(y[:, h * P:(h + 1) * P], gelu_t[:, b, c, h * P:(h + 1) * P],
                                       block_w[:, r % BLOCKS, H + c * P:H + (c + 1) * P],
                                       start=(c == 0), stop=(c == C - 1))
                mm.then_inc(y_done, 1)

            def tile(i, r):
                turn(i + 1, (r + 1) % RING)
                layer1(i, r)
                layer2(i - 1, (r - 1) % RING)

            turn(0, 0)
            turn(1, 1)
            layer1(0, 0)
            tiles(pe, 1, NT - 1, tile)
            layer1(NT - 1, (NT - 1) % RING)
            layer2(NT - 2, (NT - 2) % RING)
            layer2(NT - 1, (NT - 1) % RING)

        @block.scalar
        def _(act):
            def step(s, b):
                if live(s - 2):
                    act.wait_ge(gap_ready, s - 1)
                    after(act, rows_ready, s - 2)
                    act.activation(half_tanh[:], gap[:], ACT.Tanh, scale=0.5).then_inc(tanh_ready, 1)
                if live(s - 1):
                    act.wait_ge(gnn_done, s)
                    after(act, gnn_turned, s - 1)
                    act.activation(gnn_t[:], ps_a[:], ACT.Identity,
                                   bias=vec_cols[:, GB2:GB2 + 1]).then_inc(gnn_copied, 1)
                if live(s + 2):
                    act.wait_ge(agg_done, s + 3)
                    after(act, h_done, C * (s + 1))
                    act.copy(agg[:, b, :], ps_b[:]).then_inc(agg_copied, 1)
                if live(s):
                    act.wait_ge(spread_done, s + 1)
                    after(act, normed_ready, C * s)
                    act.copy(rrms_all[:], ps_c[:]).then_inc(spread_copied, 1)

                def hidden_chunk(c):
                    act.wait_ge(h_done, C * (s + 1) + c + 1)
                    if c == 0:
                        after(act, normed_ready, C * s)
                        after(act, sq_sum_ready, s + 1)
                    act.activation(h_bias[:, 1 - b, c, :], ps_h[:, c, :], ACT.Identity,
                                   bias=vec_cols[:, GB1 + c:GB1 + c + 1]).then_inc(h_copied, 1)
                    act.activation(squares[:, c, :], ps_h[:, c, :], ACT.Square,
                                   bias=vec_cols[:, GB1 + c:GB1 + c + 1]).then_inc(squares_ready, 1)

                def silu_chunk(c):
                    act.wait_ge(normed_ready, C * s + c + 1)
                    if c == 0:
                        after(act, gnn_done, s)
                    act.activation(hidden[:, c, :], normed[:, c, :], ACT.Silu,
                                   scale=vec_cols[:, GRW + c:GRW + c + 1]).then_inc(hidden_ready, 1)

                for work, group, c in (
                    (hidden_chunk, s + 1, 0), (hidden_chunk, s + 1, 1), (silu_chunk, s, 0),
                    (hidden_chunk, s + 1, 2), (silu_chunk, s, 1), (hidden_chunk, s + 1, 3),
                ):
                    if live(group):
                        work(c)
                if live(s - 1):
                    act.wait_ge(xn2_turned, s)
                    after(act, logits_done, s - 1)
                    act.copy(xn2_t[:], ps_b[:]).then_inc(xn2_copied, 1)
                if live(s):
                    silu_chunk(2)
                    silu_chunk(3)

            act.wait_ge(dve_consts, 3)
            steps(act, step)

            def copy_slots(i, r):
                act.wait_ge(slots_turned, i + 1)
                if not isinstance(i, int) or i >= 2:
                    act.wait_ge(fh_done, 2 * (i - 1))
                act.copy(slot_t[:, r % 2, :], (ps_a, ps_d)[r % 2][:, 0:SLOTS]).then_inc(slots_copied, 1)

            def gelu(i, r):
                b = r % 2
                if not isinstance(i, int) or i >= 2:
                    act.wait_ge(y_done, i - 1)
                for c in range(C):
                    act.wait_ge(fh_done, 2 * i + c // 2 + 1)
                    act.activation(gelu_t[:, b, c, :],
                                   ps_h[:, 2 * b + c // 2, (c % 2) * SLOTS:(c % 2 + 1) * SLOTS], ACT.Gelu,
                                   bias=block_w[:, r % BLOCKS, OB1 + c:OB1 + c + 1]).then_inc(gelu_ready, 1)

            def tile(i, r):
                copy_slots(i + 1, (r + 1) % RING)
                gelu(i, r)

            copy_slots(0, 0)
            tiles(act, 0, NT - 1, tile)
            gelu(NT - 1, (NT - 1) % RING)

        @block.vector
        def _(dve):
            dve.wait_ge(consts_loaded, 16 * 6)
            dve.wait_ge(pool_consts, 4)
            dve.wait_ge(vecs_turned, 1)
            dve.tensor_copy(vec_cols[:], ps_d[:, 0:NV]).then_inc(dve_consts, 1)
            dve.tensor_scalar(eps_ident[:], ident[:], eps_col[:, 0:1], None, ALU.mult).then_inc(dve_consts, 1)
            for k in range(TOP_K):
                dve.tensor_scalar(region_base[:, k * E:(k + 1) * E], expert_no[:], float(REGION),
                                  float(k * E * REGION), ALU.mult, ALU.add)
                m = dve.tensor_scalar(next_row[:, k * E:(k + 1) * E], expert_no[:], float(REGION),
                                      float(k * E * REGION), ALU.mult, ALU.add)
            m.then_inc(dve_consts, 1)

            def layer_norm_stats(source, stats, mv, var, chain):
                for j in range(JT):
                    m = dve.bn_stats(stats[:, j, :], source(j))
                chain.link(m, wait_apart)
                for j in range(JT):
                    m = dve.bn_aggr(mv[:, j, :], stats[:, j, :])
                chain.link(m)
                return dve.tensor_scalar(var[:], mv[:, :, 1], LN_EPS, None, ALU.add)

            def rows_of(t, j):
                return xs[:, bass.ds(t * JT + j, 1), :].rearrange("p a d -> p (a d)")

            def step(s, b):
                if live(s):
                    dve.wait_ge(squares_ready, C * s + C)
                    chain = Chain(dve, sq_chain, s)
                    chain.link(dve.tensor_tensor(sq_pair[:], squares[:, 0:2, :], squares[:, 2:4, :], ALU.add))
                    after(dve, ms_done, s)
                    dve.tensor_tensor(sq_sum[:], sq_pair[:, 0, :], sq_pair[:, 1, :],
                                      ALU.add).then_inc(sq_sum_ready, 1)
                if live(s - 2):
                    chain = Chain(dve, gate_chain, (s - 2) * 4)
                    dve.wait_ge(logits_done, s - 1)
                    chain.link(dve.tensor_tensor(
                        logits[:], ps_d[:, LG:LG + JT * E].rearrange("p (j e) -> p j e", j=JT),
                        bg_all[:].rearrange("p (a e) -> p a e", a=1).to_broadcast([P, JT, E]), ALU.add),
                        wait_apart)
                    for j in range(JT):
                        m = dve.max(top_vals[:, j, :], logits[:, j, :])
                    chain.link(m, wait_apart)
                    for j in range(JT):
                        m = dve.max_index(top_idx[:, j, :], top_vals[:, j, :], logits[:, j, :])
                    after(dve, tanh_ready, s - 2)
                    dve.tensor_tensor(gap[:], top_vals[:, :, 0], top_vals[:, :, 1],
                                      ALU.subtract).then_inc(gap_ready, 1)
                    chain.link(m)
                    chain.link(dve.tensor_copy(top_no[:], top_idx[:, :, 0:TOP_K]))
                    after(dve, prefix_done, s - 3)
                    for k in range(TOP_K):
                        m = dve.tensor_tensor(
                            chosen[:, b, :].rearrange("p (j k e) -> p j k e", j=JT, k=TOP_K)[:, :, k, :],
                            top_no[:, :, k:k + 1].to_broadcast([P, JT, E]),
                            expert_no[:].rearrange("p (a e) -> p a e", a=1).to_broadcast([P, JT, E]),
                            ALU.is_equal)
                    m.then_inc(chosen_ready, 1)
                if live(s):
                    dve.wait_ge(ms_done, s + 1)
                    after(dve, rrms_ready, s)
                    dve.tensor_scalar(mean_sq[:], ps_d[:, MS:MS + JT], 1.0 / H, RMS_EPS,
                                      ALU.mult, ALU.add).then_inc(ms_ready, 1)
                if live(s + 3):
                    wait_apart(dve, x_loaded[1 - b], 8 * (s + 3 - (1 - b)) + 16)
                    after(dve, rstd1_ready, s + 3)
                    layer_norm_stats(lambda j: rows_of(s + 3, j), stats1, mv1, var1,
                                     Chain(dve, ln1_chain, (s + 3) * 2)).then_inc(var1_ready, 1)
                if live(s):
                    dve.wait_ge(rrms_ready, s + 1)
                    after(dve, spread_done, s)
                    dve.tensor_tensor(
                        rrms_diag[:], ident[:].rearrange("p (a n) -> p a n", a=1).to_broadcast([P, JT, P]),
                        rrms[:].rearrange("p (j a) -> p j a", a=1).to_broadcast([P, JT, P]),
                        ALU.mult).then_inc(diag_ready, 1)
                if live(s - 2):
                    chain = Chain(dve, row_chain, (s - 2) * 4)
                    dve.wait_ge(prefix_done, s - 1)
                    chain.link(dve.tensor_tensor(
                        row_cand[:], ps_d[:, PR:PR + JT * KE].rearrange("p (j g) -> p j g", j=JT),
                        next_row[:].rearrange("p (a g) -> p a g", a=1).to_broadcast([P, JT, KE]), ALU.add))
                    dve.tensor_tensor(next_row[:], next_row[:], ps_d[:, TO:TO + KE],
                                      ALU.add).then_inc(prefix_read, 1)
                    chain.link(dve.tensor_tensor(
                        row_cand[:], row_cand[:], chosen[:, b, :].rearrange("p (j g) -> p j g", j=JT),
                        ALU.mult))
                    chain.link(dve.tensor_reduce(
                        row_f[:], row_cand[:].rearrange("p j (k e) -> p (j k) e", k=TOP_K), AX.X, ALU.add))
                    dve.wait_ge(tanh_ready, s - 1)
                    for k in range(TOP_K):
                        dve.tensor_scalar(payload[:, b, :, WEIGHT + k], half_tanh[:], 0.5 - k, 0.5,
                                          ALU.mult, ALU.add)
                    dve.tensor_copy(payload[:, b, :, TOKEN].bitcast(I32), token_no[:])
                    chain.link(dve.tensor_copy(row_idx[:, b, :], row_f[:]))
                    dve.tensor_scalar(token_no[:], token_no[:], float(GROUP), None,
                                      ALU.add).then_inc(rows_ready, 1)
                if live(s - 1):
                    dve.wait_ge(gnn_turned, s)
                    x2 = xs[:, bass.ds((s - 1) * JT, JT), :]
                    dve.tensor_tensor(x2, x2, ps_a[:].rearrange("p (j d) -> p j d", j=JT),
                                      ALU.add).then_inc(x2_ready, 1)
                    wait_apart(dve, x2_ready, s)
                    after(dve, rstd2_ready, s - 1)
                    layer_norm_stats(lambda j: rows_of(s - 1, j), stats2, mv2, var2,
                                     Chain(dve, ln2_chain, (s - 1) * 2)).then_inc(var2_ready, 1)

                def normed_chunk(c):
                    dve.tensor_tensor(normed[:, c, :], h_bias[:, b, c, :], rrms_all[:],
                                      ALU.mult).then_inc(normed_ready, 1)

                if live(s):
                    dve.wait_ge(h_copied, C * s + C)
                    dve.wait_ge(spread_copied, s + 1)
                    after(dve, hidden_ready, C * s)
                    normed_chunk(0)
                    normed_chunk(1)
                if live(s - 1):
                    dve.wait_ge(rstd2_ready, s)
                    after(dve, dispatched[1 - b], 8 * JT * TOP_K * (s - 2 + b))
                    for j in range(JT):
                        m = dve.tensor_scalar(payload[:, 1 - b, j, 0:P], rows_of(s - 1, j),
                                              mv2[:, j, 0:1], rstd2[:, j:j + 1], ALU.subtract, ALU.mult)
                    m.then_inc(xn2_ready, 1)
                if live(s):
                    normed_chunk(2)
                    normed_chunk(3)
                if live(s + 3):
                    dve.wait_ge(rstd1_ready, s + 4)
                    after(dve, agg_done, s + 2)
                    for j in range(JT):
                        m = dve.tensor_scalar(xn[:, 1 - b, j, :], rows_of(s + 3, j),
                                              mv1[:, j, 0:1], rstd1[:, j:j + 1], ALU.subtract, ALU.mult)
                    m.then_inc(xn_ready, 1)

            dve.wait_ge(dve_consts, 3)
            steps(dve, step)

            chain = Chain(dve, table_chain, 0)
            dve.wait_ge(rows_ready, G)
            chain.link(dve.tensor_copy(region_end[:], next_row[:]))
            dve.memset(zeros_e[:], 0.0).then_inc(ends_ready, 1)
            chain.link(dve.tensor_tensor(tiles_f[:], next_row[:], region_base[:], ALU.subtract))
            chain.link(dve.tensor_scalar(count_i[:], tiles_f[:], float(SLOTS - 1), None, ALU.add))
            chain.link(dve.tensor_scalar(tiles_i[:], count_i[:], SLOTS.bit_length() - 1, None,
                                         ALU.logical_shift_right))
            chain.link(dve.tensor_copy(tiles_f[:], tiles_i[:]))
            dve.tensor_scalar(skip[:], tiles_f[:], -float(SLOTS), float(REGION), ALU.mult, ALU.add)
            for k in range(TOP_K):
                m = dve.tensor_tensor_scan(tiles_cum[:, k * E:(k + 1) * E], tiles_f[:, k * E:(k + 1) * E],
                                           zeros_e[:], 0.0, ALU.add, ALU.add)
            chain.link(m)
            for k in range(TOP_K):
                ks = slice(k * E, (k + 1) * E)
                tab = slice(k * TILES, (k + 1) * TILES)
                chain.link(dve.tensor_tensor(
                    passed[:], tiles_cum[:, ks].rearrange("p (a e) -> p a e", a=1).to_broadcast([P, TILES, E]),
                    tile_no[:].rearrange("p (i a) -> p i a", a=1).to_broadcast([P, TILES, E]), ALU.is_le))
                dve.tensor_reduce(tile_expert[:], passed[:], AX.X, ALU.add)
                chain.link(dve.tensor_tensor(
                    skipped[:], passed[:],
                    skip[:, ks].rearrange("p (a e) -> p a e", a=1).to_broadcast([P, TILES, E]), ALU.mult))
                chain.link(dve.tensor_reduce(tile_row[:], skipped[:], AX.X, ALU.add))
                chain.link(dve.scalar_tensor_tensor(tile_row[:], tile_no[:], float(SLOTS), tile_row[:],
                                                    ALU.mult, ALU.add))
                chain.link(dve.tensor_scalar(over[:], tile_expert[:], float(E), float(DUMMY),
                                             ALU.is_ge, ALU.mult))
                chain.link(dve.scalar_tensor_tensor(tile_row[:], tile_row[:], float(k * E * REGION), over[:],
                                                    ALU.add, ALU.add))
                dve.tensor_scalar(expert_tab[:, tab], tile_expert[:], float(E - 1), float(BLOCK), ALU.min, ALU.mult)
                chain.link(dve.tensor_scalar(row_tab[:, tab], tile_row[:], float(DUMMY), None, ALU.min))
            dve.wait_ge(experts_loaded, 16 * 3 * E)
            dve.tensor_copy(experts[:].rearrange("p (e w) -> p e w", e=E)[:, :, OB1:OB1 + C],
                            vec_cols[:, FB1:FB1 + E * C].rearrange("p (e c) -> p e c", e=E)
                            ).then_inc(tables_ready, 1)
            dve.wait_ge(tables_ready, 1)

            def copy_block(i, r):
                after(dve, y_done, i - BLOCKS + 1)
                at = dve.value_load(expert_tab[0:1, bass.ds(i, 1)], min_val=0, max_val=(E - 1) * BLOCK)
                dve.tensor_copy(block_w[:, r % BLOCKS, :], experts[:, bass.ds(at, BLOCK)]).then_inc(block_ready, 1)

            def finish(i, r, k):
                y = (ps_b, ps_c)[r % 2]
                dve.wait_ge(y_done, i + 1)
                dve.tensor_tensor(
                    y_bias[:, r, :, :], y[:, 0:SLOTS].rearrange("p (h d) -> p h d", h=HT),
                    block_w[:, r % BLOCKS, OB2:OB2 + P].rearrange("p (a d) -> p a d", a=1).to_broadcast([P, HT, P]),
                    ALU.add).then_inc(y_chain, 1)
                dve.wait_ge(y_chain, i + 1)
                if not isinstance(i, int) or i >= RING:
                    dve.wait_ge(added[r], 16 * HT // RING * (i - r))
                dve.tensor_tensor(y_out[:, r, :, :], y_bias[:, r, :, :],
                                  slot_rows[:, r, :, WEIGHT + k:WEIGHT + k + 1].to_broadcast([P, HT, P]),
                                  ALU.mult).then_inc(y_ready, 1)

            copy_block(0, 0)
            copy_block(1, 1)
            tiles(dve, 0, TILES, lambda i, r: (copy_block(i + 2, (r + 2) % RING), finish(i, r, 0)))
            tiles(dve, TILES, NT - 2, lambda i, r: (copy_block(i + 2, (r + 2) % RING), finish(i, r, 1)))
            finish(NT - 2, (NT - 2) % RING, 1)
            finish(NT - 1, (NT - 1) % RING, 1)


_IN = ["x", "adj_t", "epsilon", "g_w1", "vectors", "g_w2", "f_wg", "f_bg", "f_w1", "f_w2", "f_b2"]


def kernel(x, adj, L0_gnn_epsilon, L0_gnn_W1, L0_gnn_b1, L0_gnn_rms_weight, L0_gnn_W2, L0_gnn_b2,
           L0_ffn_Wg, L0_ffn_bg, L0_ffn_W1, L0_ffn_b1, L0_ffn_W2, L0_ffn_b2):
    import concourse.bacc as bacc
    from concourse.bass_utils import run_bass_kernel_spmd

    B, N, D = x.shape
    E = L0_ffn_Wg.shape[1]
    given = {
        "x": np.asarray(x).reshape(B * N, D),
        "adj_t": np.asarray(adj).transpose(0, 2, 1),
        "epsilon": np.asarray(L0_gnn_epsilon).reshape(1, 1),
        "g_w1": L0_gnn_W1,
        "vectors": np.concatenate([np.asarray(a).reshape(-1, D) for a in
                                   (L0_gnn_b1, L0_gnn_rms_weight, L0_gnn_b2, L0_ffn_b1)]),
        "g_w2": L0_gnn_W2,
        "f_wg": L0_ffn_Wg,
        "f_bg": np.asarray(L0_ffn_bg).reshape(1, E),
        "f_w1": L0_ffn_W1,
        "f_w2": L0_ffn_W2,
        "f_b2": L0_ffn_b2,
    }
    nc = bacc.Bacc("TRN2", target_bir_lowering=False, num_devices=1)
    arrays, args = {}, []
    for name in _IN:
        a = np.ascontiguousarray(given[name])
        arrays[f"in_{name}"] = a
        args.append(nc.dram_tensor(f"in_{name}", a.shape, mybir.dt.from_np(a.dtype), kind="ExternalInput").ap())
    out = nc.dram_tensor("out_y", (B * N, D), F32, kind="ExternalOutput").ap()
    moe_gnn(nc, *args, out)
    r = run_bass_kernel_spmd(nc, [arrays], core_ids=[0])
    return r.results[0]["out_y"].reshape(B, N, D)
```

```python
from contextlib import ExitStack

import numpy as np

import concourse.bass as bass
from concourse import mybir

F32 = mybir.dt.float32
BF16 = mybir.dt.bfloat16
I32 = mybir.dt.int32
U32 = mybir.dt.uint32
ALU = mybir.AluOpType
ACT = mybir.ActivationFunctionType
AX = mybir.AxisListType

P = 128
JT = 4
GROUP = JT * P
SLOTS = 256
HT = SLOTS // P
TOP_K = 2
RING = 8
PAYLOADS = 4
BLOCKS = 4
LN_EPS = 1e-5
RMS_EPS = 1e-6

TOKEN, WEIGHT, ROW = P, P + 1, P + 3


class Chain:

    def __init__(self, engine, sem, done):
        self.engine, self.sem, self.done, self.n = engine, sem, done, 0

    def link(self, instruction, wait=None):
        self.n += 1
        instruction.then_inc(self.sem, 1)
        if wait:
            wait(self.engine, self.sem, self.done + self.n)
        else:
            self.engine.wait_ge(self.sem, self.done + self.n)


def moe_gnn(nc, x, adj_t, epsilon, g_w1, vectors, g_w2, f_wg, f_bg, f_w1, f_w2, f_b2, out):
    T, D = x.shape
    H = g_w1.shape[1]
    E = f_wg.shape[1]
    NODES = adj_t.shape[1]
    C = H // P
    G = T // GROUP
    BPT = P // NODES
    KE = TOP_K * E
    REGION = T + SLOTS
    DUMMY = KE * REGION
    TILES = (T + E * (SLOTS - 1)) // SLOTS
    NT = TOP_K * TILES
    BLOCK = 2 * C * P + C + P
    OB1, OB2 = 2 * C * P, 2 * C * P + C
    NV = vectors.shape[0]
    GB1, GRW, GB2, FB1 = 0, C, 2 * C, 2 * C + 1
    assert D == P and C == 4 and BPT == 2 and G % 4 == 0 and G > 8 and TILES % 2 == 1 and HT == 2

    with ExitStack() as ctx:
        def sb(name, shape, dt=F32):
            return ctx.enter_context(nc.sbuf_tensor(name, shape, dt))

        def sem(name):
            return ctx.enter_context(nc.semaphore(name))

        rows = nc.dram_tensor("dispatched_rows", (DUMMY + SLOTS, ROW), F32).ap()

        ident = sb("ident", [P, P])
        eps_ident = sb("eps_ident", [P, P])
        ones = sb("ones", [P, P])
        ones_bf = sb("ones_bf", [P, P], BF16)
        before = sb("before", [P, P], BF16)
        neg_half = sb("neg_half", [P, JT])
        expert_no = sb("expert_no", [P, E])
        tile_no = sb("tile_no", [P, TILES])
        region_base = sb("region_base", [P, KE])
        token_no = sb("token_no", [P, JT], I32)
        pad_rows = sb("pad_rows", [P, HT, ROW])
        eps_col = sb("eps_col", [P, 1])
        bg_all = sb("bg_all", [P, E])
        w1g = sb("w1g", [P, H])
        w2g = sb("w2g", [P, C, P])
        wg = sb("wg", [P, E])
        vec_rows = sb("vec_rows", [NV, P])
        vec_cols = sb("vec_cols", [P, NV])
        experts = sb("experts", [P, E * BLOCK])

        xs = sb("xs", [P, G * JT, P])
        adj_blocks = sb("adj_blocks", [P, 2, JT, P])
        stats1 = sb("stats1", [P, JT, 6])
        stats2 = sb("stats2", [P, JT, 6])
        mv1 = sb("mv1", [P, JT, 2])
        mv2 = sb("mv2", [P, JT, 2])
        var1 = sb("var1", [P, JT])
        var2 = sb("var2", [P, JT])
        rstd1 = sb("rstd1", [P, JT])
        rstd2 = sb("rstd2", [P, JT])
        xn = sb("xn", [P, 2, JT, P])
        agg = sb("agg", [P, 2, GROUP])
        h_bias = sb("h_bias", [P, 2, C, GROUP])
        squares = sb("squares", [P, C, GROUP])
        sq_pair = sb("sq_pair", [P, 2, GROUP])
        sq_sum = sb("sq_sum", [P, GROUP])
        mean_sq = sb("mean_sq", [P, JT])
        rrms = sb("rrms", [P, JT])
        rrms_diag = sb("rrms_diag", [P, JT, P])
        rrms_all = sb("rrms_all", [P, GROUP])
        normed = sb("normed", [P, C, GROUP])
        hidden = sb("hidden", [P, C, GROUP])
        gnn_t = sb("gnn_t", [P, GROUP])
        payload = sb("payload", [P, PAYLOADS, JT, ROW])
        xn2_t = sb("xn2_t", [P, GROUP])
        logits = sb("logits", [P, JT, E])
        top_vals = sb("top_vals", [P, JT, 8])
        top_idx = sb("top_idx", [P, JT, 8], U32)
        top_no = sb("top_no", [P, JT, TOP_K])
        gap = sb("gap", [P, JT])
        half_tanh = sb("half_tanh", [P, JT])
        chosen = sb("chosen", [P, 2, JT * KE], BF16)
        next_row = sb("next_row", [P, KE])
        row_cand = sb("row_cand", [P, JT, KE])
        row_f = sb("row_f", [P, JT * TOP_K])
        row_idx = sb("row_idx", [P, 2, JT * TOP_K], I32)

        region_end = sb("region_end", [P, KE], I32)
        count_i = sb("count_i", [P, KE], I32)
        tiles_i = sb("tiles_i", [P, KE], I32)
        tiles_f = sb("tiles_f", [P, KE])
        zeros_e = sb("zeros_e", [P, E])
        tiles_cum = sb("tiles_cum", [P, KE])
        skip = sb("skip", [P, KE])
        passed = sb("passed", [P, TILES, E])
        skipped = sb("skipped", [P, TILES, E])
        tile_expert = sb("tile_expert", [P, TILES])
        tile_row = sb("tile_row", [P, TILES])
        over = sb("over", [P, TILES])
        expert_tab = sb("expert_tab", [P, NT], I32)
        row_tab = sb("row_tab", [P, NT], I32)

        slot_rows = sb("slot_rows", [P, RING, HT, ROW])
        slot_t = sb("slot_t", [P, 2, SLOTS])
        block_w = sb("block_w", [P, BLOCKS, BLOCK])
        gelu_t = sb("gelu_t", [P, 2, C, SLOTS])
        y_bias = sb("y_bias", [P, 2, HT, P])
        y_out = sb("y_out", [P, RING, HT, P])

        ps_h = ctx.enter_context(nc.psum_tensor("ps_h", [P, C, 512], F32))
        ps_a = ctx.enter_context(nc.psum_tensor("ps_a", [P, 512], F32))
        ps_b = ctx.enter_context(nc.psum_tensor("ps_b", [P, 512], F32))
        ps_c = ctx.enter_context(nc.psum_tensor("ps_c", [P, 512], F32))
        ps_d = ctx.enter_context(nc.psum_tensor("ps_d", [P, 512], F32))
        LG, PR, TO = 0, 64, 192

        consts_loaded = sem("consts_loaded")
        experts_loaded = sem("experts_loaded")
        pool_consts = sem("pool_consts")
        dve_consts = sem("dve_consts")
        vecs_turned = sem("vecs_turned")
        x_loaded = [sem(f"x_loaded{b}") for b in range(2)]
        adj_loaded = [sem(f"adj_loaded{b}") for b in range(2)]
        ln1_chain = sem("ln1_chain")
        var1_ready = sem("var1_ready")
        rstd1_ready = sem("rstd1_ready")
        xn_ready = sem("xn_ready")
        agg_done = sem("agg_done")
        agg_copied = sem("agg_copied")
        h_done = sem("h_done")
        h_copied = sem("h_copied")
        squares_ready = sem("squares_ready")
        sq_chain = sem("sq_chain")
        sq_sum_ready = sem("sq_sum_ready")
        ms_done = sem("ms_done")
        ms_ready = sem("ms_ready")
        rrms_ready = sem("rrms_ready")
        diag_ready = sem("diag_ready")
        spread_done = sem("spread_done")
        spread_copied = sem("spread_copied")
        normed_ready = sem("normed_ready")
        hidden_ready = sem("hidden_ready")
        gnn_done = sem("gnn_done")
        gnn_copied = sem("gnn_copied")
        gnn_turned = sem("gnn_turned")
        x2_ready = sem("x2_ready")
        x2_stored = sem("x2_stored")
        ln2_chain = sem("ln2_chain")
        var2_ready = sem("var2_ready")
        rstd2_ready = sem("rstd2_ready")
        xn2_ready = sem("xn2_ready")
        xn2_turned = sem("xn2_turned")
        xn2_copied = sem("xn2_copied")
        logits_done = sem("logits_done")
        gate_chain = sem("gate_chain")
        gap_ready = sem("gap_ready")
        tanh_ready = sem("tanh_ready")
        chosen_ready = sem("chosen_ready")
        prefix_done = sem("prefix_done")
        prefix_read = sem("prefix_read")
        row_chain = sem("row_chain")
        rows_ready = sem("rows_ready")
        dispatched = [sem(f"dispatched{b}") for b in range(2)]
        table_chain = sem("table_chain")
        ends_ready = sem("ends_ready")
        padded = sem("padded")
        tables_ready = sem("tables_ready")
        slots_loaded = [sem(f"slots_loaded{r}") for r in range(RING)]
        slots_turned = sem("slots_turned")
        slots_copied = sem("slots_copied")
        block_ready = sem("block_ready")
        fh_done = sem("fh_done")
        gelu_ready = sem("gelu_ready")
        y_done = sem("y_done")
        y_chain = sem("y_chain")
        y_ready = sem("y_ready")
        added = [sem(f"added{r}") for r in range(RING)]

        def wait_apart(engine, semaphore, value):
            if not isinstance(value, int):
                value = engine.to_reg(value)
                engine.wait_ge(pool_consts, 1)
            engine.wait_ge(semaphore, value)

        def live(t):
            return not isinstance(t, int) or 0 <= t < G

        def steps(engine, step, start, stop, loop_start, loop_stop):
            for s in range(start, loop_start):
                step(s, s % 4)
            with engine.Fori(0, (loop_stop - loop_start) // 4) as turn_no:
                for d in range(4):
                    step(turn_no * 4 + (loop_start + d), (loop_start + d) % 4)
            for s in range(loop_stop, stop):
                step(s, s % 4)

        def after(engine, semaphore, value):
            if not isinstance(value, int) or value >= 1:
                engine.wait_ge(semaphore, value)

        def tiles(engine, first, last, tile):
            start = first + (last - first) % RING
            while start < min(RING + 1, last):
                start = min(start + RING, last)
            for i in range(first, start):
                tile(i, i % RING)
            if last > start:
                with engine.Fori(0, (last - start) // RING) as turn_no:
                    for d in range(RING):
                        tile(turn_no * RING + (start + d), (start + d) % RING)

        x_view = x.rearrange("(r p) d -> p r d", p=P)
        out_view = out.rearrange("(r p) d -> p r d", p=P)
        adj_view = adj_t.rearrange("(r h) m n -> h m r n", h=BPT)

        block = ctx.enter_context(nc.Block())

        @block.sync
        def _(sp):
            for dst, src in (
                (w1g[:], g_w1), (w2g[:], g_w2.rearrange("(c p) d -> p c d", p=P)),
                (wg[:], f_wg), (vec_rows[:], vectors),
                (eps_col[:], epsilon.to_broadcast([P, 1])), (bg_all[:], f_bg.to_broadcast([P, E])),
            ):
                sp.dma_start(dst, src).then_inc(consts_loaded, 16)

            def load_x(t, b):
                after(sp, x_loaded[b], 8 * (t - b))
                sp.dma_start(xs[:, bass.ds(t * JT, JT), :],
                             x_view[:, bass.ds(t * JT, JT), :]).then_inc(x_loaded[b], 16)

            def load_adj(t, b):
                for h in range(BPT):
                    half = slice(h * NODES, (h + 1) * NODES)
                    sp.dma_start(adj_blocks[half, b, :, half],
                                 adj_view[h, :, bass.ds(t * JT, JT), :]).then_inc(adj_loaded[b], 16)

            load_x(0, 0)
            load_x(1, 1)
            sp.wait_ge(pool_consts, 1)
            load_adj(0, 0)
            load_adj(1, 1)
            load_x(2, 0)
            load_x(3, 1)
            for e in range(E):
                blk = experts[:, e * BLOCK:(e + 1) * BLOCK]
                sp.dma_start(blk[:, 0:H], f_w1[e]).then_inc(experts_loaded, 16)
                sp.dma_start(blk[:, H:2 * H].rearrange("p (c d) -> p c d", c=C),
                             f_w2[e].rearrange("(c p) d -> p c d", p=P)).then_inc(experts_loaded, 16)
                sp.dma_start(blk[:, OB2:OB2 + P],
                             f_b2[e:e + 1, :].to_broadcast([P, P])).then_inc(experts_loaded, 16)

            def step(s, q):
                b = q % 2
                if live(s + 4) and (not isinstance(s, int) or s >= 0):
                    load_x(s + 4, b)
                if live(s + 4) and (not isinstance(s, int) or s >= -2):
                    sp.wait_ge(agg_done, s + 3)
                    load_adj(s + 4, b)
                if live(s - 1):
                    sp.wait_ge(x2_ready, s)
                    sp.dma_start(out_view[:, bass.ds((s - 1) * JT, JT), :],
                                 xs[:, bass.ds((s - 1) * JT, JT), :]).then_inc(x2_stored, 16)

            steps(sp, step, -3, G + 2, 4, G - 4)

            sp.wait_ge(pool_consts, 3)
            sp.dma_start(rows[DUMMY:DUMMY + SLOTS, :].rearrange("(h p) c -> p h c", p=P),
                         pad_rows[:]).then_inc(padded, 16)
            sp.wait_ge(ends_ready, 1)
            for g in range(KE):
                end = sp.value_load(region_end[0:1, g:g + 1], min_val=0, max_val=DUMMY - SLOTS)
                sp.dma_start(rows[bass.ds(end, SLOTS), :].rearrange("(h p) c -> p h c", p=P),
                             pad_rows[:]).then_inc(padded, 16)

            def load_slots(i, r):
                if not isinstance(i, int) or i >= RING:
                    wait_apart(sp, added[r], 16 * HT // RING * (i - r))
                start = sp.value_load(row_tab[0:1, bass.ds(i, 1)], min_val=0, max_val=DUMMY)
                sp.dma_start(slot_rows[:, r, :, :],
                             rows[bass.ds(start, SLOTS), :].rearrange("(h p) c -> p h c", p=P)
                             ).then_inc(slots_loaded[r], 16)

            sp.wait_ge(tables_ready, 1)
            sp.wait_ge(padded, 16 * (KE + 1))
            for b in range(2):
                sp.wait_ge(dispatched[b], 16 * JT * TOP_K * (G // 2))
            tiles(sp, 0, RING, load_slots)
            tiles(sp, RING, NT, load_slots)
            sp.wait_ge(x2_stored, 16 * G)
            for r in range(RING):
                sp.wait_ge(added[r], 16 * HT * len(range(r, NT, RING)))

        @block.gpsimd
        def _(pool):
            pool.memset(adj_blocks[:], 0.0).then_inc(pool_consts, 1)
            pool.memset(ident[:], 0.0)
            pool.memset(before[:], 0.0)
            pool.memset(pad_rows[:], 0.0)
            pool.memset(neg_half[:], -0.5)
            pool.memset(ones[:], 1.0)
            pool.memset(ones_bf[:], 1.0)
            pool.iota(expert_no[:], [[1, E]], base=0, channel_multiplier=0,
                      allow_small_or_imprecise_dtypes=True)
            pool.iota(tile_no[:], [[1, TILES]], base=0, channel_multiplier=0,
                      allow_small_or_imprecise_dtypes=True)
            pool.iota(token_no[:], [[P, JT]], base=0, channel_multiplier=1)
            pool.iota(top_no[:, 0, 0:1], [[1, 1]], base=0, channel_multiplier=0,
                      allow_small_or_imprecise_dtypes=True).then_inc(pool_consts, 1)
            pool.wait_ge(pool_consts, 2)
            pool.memset(pad_rows[:, :, TOKEN:TOKEN + 1].bitcast(I32), T).then_inc(pool_consts, 1)
            pool.affine_select(out=ident[:], in_=ident[:], compare_op=ALU.not_equal, fill=1.0,
                               base=0, pattern=[[-1, P]], channel_multiplier=1)
            pool.affine_select(out=before[:], in_=before[:], compare_op=ALU.is_ge, fill=1.0,
                               base=0, pattern=[[-1, P]], channel_multiplier=1).then_inc(pool_consts, 1)

            def step(s, q):
                b = q % 2
                if live(s + 3):
                    pool.wait_ge(var1_ready, s + 4)
                    after(pool, xn_ready, s + 3)
                    pool.tensor_tensor(rstd1[:], var1[:], neg_half[:],
                                       ALU.pow).then_inc(rstd1_ready, 1)
                if live(s - 4):
                    wait_apart(pool, rows_ready, s - 3)
                    for jk in range(JT * TOP_K):
                        pool.indirect_dma_start(
                            rows, bass.IndirectOffsetOnAxis(row_idx[:, b, jk:jk + 1], 0),
                            payload[:, q, jk // TOP_K, :], None).then_inc(dispatched[b], 16)
                if live(s - 1):
                    pool.wait_ge(var2_ready, s)
                    after(pool, xn2_ready, s - 1)
                    pool.tensor_tensor(rstd2[:], var2[:], neg_half[:],
                                       ALU.pow).then_inc(rstd2_ready, 1)
                if live(s + 1):
                    pool.wait_ge(ms_ready, s + 2)
                    after(pool, diag_ready, s + 1)
                    pool.tensor_tensor(rrms[:], mean_sq[:], neg_half[:],
                                       ALU.pow).then_inc(rrms_ready, 1)

            steps(pool, step, -3, G + 4, 5, G - 3)

            def add_tile(i, r):
                wait_apart(pool, y_ready, i + 1)
                for h in range(HT):
                    pool.indirect_dma_start(
                        out, bass.IndirectOffsetOnAxis(slot_rows[:, r, h, TOKEN:TOKEN + 1].bitcast(I32), 0),
                        y_out[:, r, h, :], None, bounds_check=T - 1, oob_is_err=False,
                        compute_op=ALU.add).then_inc(added[r], 16)

            pool.wait_ge(x2_stored, 16 * G)
            tiles(pool, 0, TILES, add_tile)
            for r in range(RING):
                pool.wait_ge(added[r], 16 * HT * len(range(r, TILES, RING)))
            tiles(pool, TILES, NT, add_tile)

        @block.tensor
        def _(pe):
            pe.wait_ge(consts_loaded, 16 * 6)
            pe.wait_ge(pool_consts, 4)
            pe.transpose(ps_d[:, 0:NV], vec_rows[:], ident[0:NV, 0:NV]).then_inc(vecs_turned, 1)

            def step(s, q):
                b = q % 2
                if live(s + 1):
                    pe.wait_ge(agg_copied, s + 2)
                    for c in range(C):
                        after(pe, squares_ready, C * s + c + 1)
                        pe.matmul(ps_h[:, c, :], w1g[:, c * P:(c + 1) * P], agg[:, 1 - b, :],
                                  start=True, stop=True).then_inc(h_done, 1)
                if live(s):
                    pe.wait_ge(ms_ready, s + 1)
                    pe.wait_ge(diag_ready, s + 1)
                    pe.matmul(ps_c[:], ones[:], rrms_diag[:].rearrange("p j n -> p (j n)"),
                              start=True, stop=True).then_inc(spread_done, 1)
                if live(s - 2):
                    pe.wait_ge(xn2_ready, s - 1)
                    pe.wait_ge(agg_copied, min(s + 2, G) if isinstance(s, int) else s + 2)
                    for j in range(JT):
                        mm = pe.transpose(ps_b[:, j * P:(j + 1) * P], payload[:, (q - 2) % PAYLOADS, j, 0:P],
                                          ident[:])
                    mm.then_inc(xn2_turned, 1)
                if live(s - 3):
                    pe.wait_ge(chosen_ready, s - 2)
                    ch = chosen[:, 1 - b, :]
                    W = JT * KE
                    pe.matmul(ps_d[:, PR:PR + W], before[:], ch, start=True, stop=False)
                    for d in range(1, JT):
                        pe.matmul(ps_d[:, PR + d * KE:PR + W], ones_bf[:], ch[:, 0:W - d * KE],
                                  start=False, stop=(d == JT - 1))
                    for j in range(JT):
                        mm = pe.matmul(ps_d[:, TO:TO + KE], ones_bf[:], ch[:, j * KE:(j + 1) * KE],
                                       start=(j == 0), stop=(j == JT - 1))
                    mm.then_inc(prefix_done, 1)

                def second_layer(chunks):
                    for c in chunks:
                        pe.wait_ge(hidden_ready, C * (s - 1) + c + 1)
                        mm = pe.matmul(ps_a[:], w2g[:, c, :], hidden[:, c, :],
                                       start=(c == 0), stop=(c == C - 1))
                    return mm

                if live(s - 1):
                    after(pe, x2_ready, s - 1)
                    second_layer((0, 1))
                if live(s - 2):
                    pe.wait_ge(xn2_copied, s - 1)
                    after(pe, prefix_read, s - 2)
                    for j in range(JT):
                        mm = pe.matmul(ps_d[:, LG + j * E:LG + (j + 1) * E], xn2_t[:, j * P:(j + 1) * P],
                                       wg[:], start=True, stop=True)
                    mm.then_inc(logits_done, 1)
                if live(s - 1):
                    second_layer((2, 3)).then_inc(gnn_done, 1)
                if live(s + 2):
                    pe.wait_ge(adj_loaded[b], 16 * (s + 2 - b) + 32)
                    pe.wait_ge(xn_ready, s + 3)
                    after(pe, agg_copied, s + 2)
                    after(pe, xn2_copied, s - 1)
                    for j in range(JT):
                        cols = ps_b[:, j * P:(j + 1) * P]
                        pe.matmul(cols, xn[:, b, j, :], adj_blocks[:, b, j, :], start=True, stop=False)
                        mm = pe.matmul(cols, xn[:, b, j, :], eps_ident[:], start=False, stop=True)
                    mm.then_inc(agg_done, 1)
                if live(s - 1):
                    pe.wait_ge(gnn_copied, s)
                    for j in range(JT):
                        mm = pe.transpose(ps_a[:, j * P:(j + 1) * P], gnn_t[:, j * P:(j + 1) * P], ident[:])
                    mm.then_inc(gnn_turned, 1)
                if live(s + 1):
                    pe.wait_ge(sq_sum_ready, s + 2)
                    after(pe, spread_copied, s + 1)
                    for j in range(JT):
                        mm = pe.matmul(ps_c[:, j:j + 1], sq_sum[:, j * P:(j + 1) * P],
                                       ones[:, 0:1], start=True, stop=True)
                    mm.then_inc(ms_done, 1)

            pe.wait_ge(dve_consts, 3)
            steps(pe, step, -3, G + 3, 5, G - 3)

            def turn(i, r):
                pe.wait_ge(slots_loaded[r], 16 // RING * (i - r) + 16)
                if not isinstance(i, int) or i >= 2:
                    pe.wait_ge(slots_copied, i - 1)
                for h in range(HT):
                    mm = pe.transpose((ps_a, ps_d)[r % 2][:, h * P:(h + 1) * P],
                                      slot_rows[:, r, h, 0:P], ident[:])
                mm.then_inc(slots_turned, 1)

            def layer1(i, r):
                b = r % 2
                pe.wait_ge(slots_copied, i + 1)
                pe.wait_ge(block_ready, i + 1)
                for c in range(C):
                    mm = pe.matmul(ps_h[:, 2 * b + c // 2, (c % 2) * SLOTS:(c % 2 + 1) * SLOTS],
                                   block_w[:, r % BLOCKS, c * P:(c + 1) * P], slot_t[:, b, :],
                                   start=True, stop=True)
                    if c % 2:
                        mm.then_inc(fh_done, 1)

            def layer2(i, r):
                b = r % 2
                y = (ps_b, ps_c)[b]
                pe.wait_ge(gelu_ready, C * i + C)
                if not isinstance(i, int) or i >= 2:
                    pe.wait_ge(y_chain, i - 1)
                for h in range(HT):
                    for c in range(C):
                        mm = pe.matmul(y[:, h * P:(h + 1) * P], gelu_t[:, b, c, h * P:(h + 1) * P],
                                       block_w[:, r % BLOCKS, H + c * P:H + (c + 1) * P],
                                       start=(c == 0), stop=(c == C - 1))
                mm.then_inc(y_done, 1)

            def tile(i, r):
                turn(i + 1, (r + 1) % RING)
                layer1(i, r)
                layer2(i - 1, (r - 1) % RING)

            turn(0, 0)
            turn(1, 1)
            layer1(0, 0)
            tiles(pe, 1, NT - 1, tile)
            layer1(NT - 1, (NT - 1) % RING)
            layer2(NT - 2, (NT - 2) % RING)
            layer2(NT - 1, (NT - 1) % RING)

        @block.scalar
        def _(act):
            def step(s, q):
                b = q % 2

                def hidden_chunk(c):
                    act.wait_ge(h_done, C * (s + 1) + c + 1)
                    if c == 0:
                        after(act, normed_ready, C * s)
                        after(act, sq_sum_ready, s + 1)
                    act.activation(h_bias[:, 1 - b, c, :], ps_h[:, c, :], ACT.Identity,
                                   bias=vec_cols[:, GB1 + c:GB1 + c + 1]).then_inc(h_copied, 1)
                    act.activation(squares[:, c, :], ps_h[:, c, :], ACT.Square,
                                   bias=vec_cols[:, GB1 + c:GB1 + c + 1]).then_inc(squares_ready, 1)

                def silu_chunk(c):
                    act.wait_ge(normed_ready, C * s + c + 1)
                    if c == 0:
                        after(act, gnn_done, s)
                    act.activation(hidden[:, c, :], normed[:, c, :], ACT.Silu,
                                   scale=vec_cols[:, GRW + c:GRW + c + 1]).then_inc(hidden_ready, 1)

                if live(s + 1):
                    hidden_chunk(0)
                    hidden_chunk(1)
                if live(s - 3):
                    act.wait_ge(gap_ready, s - 2)
                    after(act, rows_ready, s - 3)
                    act.activation(half_tanh[:], gap[:], ACT.Tanh, scale=0.5).then_inc(tanh_ready, 1)
                if live(s + 1):
                    hidden_chunk(2)
                if live(s):
                    act.wait_ge(spread_done, s + 1)
                    after(act, normed_ready, C * s)
                    act.copy(rrms_all[:], ps_c[:]).then_inc(spread_copied, 1)
                if live(s - 2):
                    act.wait_ge(xn2_turned, s - 1)
                    after(act, logits_done, s - 2)
                    act.copy(xn2_t[:], ps_b[:]).then_inc(xn2_copied, 1)
                if live(s + 1):
                    hidden_chunk(3)
                if live(s - 1):
                    act.wait_ge(gnn_done, s)
                    after(act, gnn_turned, s - 1)
                    act.activation(gnn_t[:], ps_a[:], ACT.Identity,
                                   bias=vec_cols[:, GB2:GB2 + 1]).then_inc(gnn_copied, 1)
                if live(s):
                    silu_chunk(0)
                    silu_chunk(1)
                    silu_chunk(2)
                if live(s + 2):
                    act.wait_ge(agg_done, s + 3)
                    after(act, h_done, C * (s + 1))
                    act.copy(agg[:, b, :], ps_b[:]).then_inc(agg_copied, 1)
                if live(s):
                    silu_chunk(3)

            act.wait_ge(dve_consts, 3)
            steps(act, step, -3, G + 3, 5, G - 3)

            def copy_slots(i, r):
                act.wait_ge(slots_turned, i + 1)
                if not isinstance(i, int) or i >= 2:
                    act.wait_ge(fh_done, 2 * (i - 1))
                act.copy(slot_t[:, r % 2, :], (ps_a, ps_d)[r % 2][:, 0:SLOTS]).then_inc(slots_copied, 1)

            def gelu(i, r):
                b = r % 2
                if not isinstance(i, int) or i >= 2:
                    act.wait_ge(y_done, i - 1)
                for c in range(C):
                    act.wait_ge(fh_done, 2 * i + c // 2 + 1)
                    act.activation(gelu_t[:, b, c, :],
                                   ps_h[:, 2 * b + c // 2, (c % 2) * SLOTS:(c % 2 + 1) * SLOTS], ACT.Gelu,
                                   bias=block_w[:, r % BLOCKS, OB1 + c:OB1 + c + 1]).then_inc(gelu_ready, 1)

            def tile(i, r):
                copy_slots(i + 1, (r + 1) % RING)
                gelu(i, r)

            copy_slots(0, 0)
            tiles(act, 0, NT - 1, tile)
            gelu(NT - 1, (NT - 1) % RING)

        @block.vector
        def _(dve):
            dve.wait_ge(consts_loaded, 16 * 6)
            dve.wait_ge(pool_consts, 4)
            dve.wait_ge(vecs_turned, 1)
            dve.tensor_copy(vec_cols[:], ps_d[:, 0:NV]).then_inc(dve_consts, 1)
            dve.tensor_scalar(eps_ident[:], ident[:], eps_col[:, 0:1], None, ALU.mult).then_inc(dve_consts, 1)
            for k in range(TOP_K):
                dve.tensor_scalar(region_base[:, k * E:(k + 1) * E], expert_no[:], float(REGION),
                                  float(k * E * REGION), ALU.mult, ALU.add)
                m = dve.tensor_scalar(next_row[:, k * E:(k + 1) * E], expert_no[:], float(REGION),
                                      float(k * E * REGION), ALU.mult, ALU.add)
            m.then_inc(dve_consts, 1)

            def layer_norm_stats(source, stats, mv, var, chain):
                for j in range(JT):
                    m = dve.bn_stats(stats[:, j, :], source(j))
                chain.link(m, wait_apart)
                for j in range(JT):
                    m = dve.bn_aggr(mv[:, j, :], stats[:, j, :])
                chain.link(m)
                return dve.tensor_scalar(var[:], mv[:, :, 1], LN_EPS, None, ALU.add)

            def rows_of(t, j):
                return xs[:, bass.ds(t * JT + j, 1), :].rearrange("p a d -> p (a d)")

            def step(s, q):
                b = q % 2
                if live(s + 3):
                    wait_apart(dve, x_loaded[1 - b], 8 * (s + 3 - (1 - b)) + 16)
                    after(dve, rstd1_ready, s + 3)
                    layer_norm_stats(lambda j: rows_of(s + 3, j), stats1, mv1, var1,
                                     Chain(dve, ln1_chain, (s + 3) * 2)).then_inc(var1_ready, 1)
                if live(s - 3):
                    ranks = Chain(dve, row_chain, (s - 3) * 4)
                    dve.wait_ge(prefix_done, s - 2)
                    ranks.link(dve.tensor_tensor(
                        row_cand[:], ps_d[:, PR:PR + JT * KE].rearrange("p (j g) -> p j g", j=JT),
                        next_row[:].rearrange("p (a g) -> p a g", a=1).to_broadcast([P, JT, KE]), ALU.add))
                    dve.tensor_tensor(next_row[:], next_row[:], ps_d[:, TO:TO + KE],
                                      ALU.add).then_inc(prefix_read, 1)
                def normed_chunk(c):
                    dve.tensor_tensor(normed[:, c, :], h_bias[:, b, c, :], rrms_all[:],
                                      ALU.mult).then_inc(normed_ready, 1)

                if live(s):
                    dve.wait_ge(h_copied, C * s + C)
                    dve.wait_ge(spread_copied, s + 1)
                    after(dve, hidden_ready, C * s)
                    for c in range(C):
                        normed_chunk(c)
                if live(s + 1):
                    dve.wait_ge(squares_ready, C * (s + 1) + C)
                    chain = Chain(dve, sq_chain, s + 1)
                    chain.link(dve.tensor_tensor(sq_pair[:], squares[:, 0:2, :], squares[:, 2:4, :], ALU.add))
                    after(dve, ms_done, s + 1)
                    dve.tensor_tensor(sq_sum[:], sq_pair[:, 0, :], sq_pair[:, 1, :],
                                      ALU.add).then_inc(sq_sum_ready, 1)
                if live(s + 3):
                    dve.wait_ge(rstd1_ready, s + 4)
                    after(dve, agg_done, s + 2)
                    for j in range(JT):
                        m = dve.tensor_scalar(xn[:, 1 - b, j, :], rows_of(s + 3, j),
                                              mv1[:, j, 0:1], rstd1[:, j:j + 1], ALU.subtract, ALU.mult)
                    m.then_inc(xn_ready, 1)
                if live(s - 2):
                    chain = Chain(dve, gate_chain, (s - 2) * 4)
                    dve.wait_ge(logits_done, s - 1)
                    chain.link(dve.tensor_tensor(
                        logits[:], ps_d[:, LG:LG + JT * E].rearrange("p (j e) -> p j e", j=JT),
                        bg_all[:].rearrange("p (a e) -> p a e", a=1).to_broadcast([P, JT, E]), ALU.add),
                        wait_apart)
                    for j in range(JT):
                        m = dve.max(top_vals[:, j, :], logits[:, j, :])
                    chain.link(m, wait_apart)
                    for j in range(JT):
                        m = dve.max_index(top_idx[:, j, :], top_vals[:, j, :], logits[:, j, :])
                    after(dve, tanh_ready, s - 2)
                    dve.tensor_tensor(gap[:], top_vals[:, :, 0], top_vals[:, :, 1],
                                      ALU.subtract).then_inc(gap_ready, 1)
                    chain.link(m)
                    chain.link(dve.tensor_copy(top_no[:], top_idx[:, :, 0:TOP_K]))
                    after(dve, prefix_done, s - 3)
                    for k in range(TOP_K):
                        m = dve.tensor_tensor(
                            chosen[:, b, :].rearrange("p (j k e) -> p j k e", j=JT, k=TOP_K)[:, :, k, :],
                            top_no[:, :, k:k + 1].to_broadcast([P, JT, E]),
                            expert_no[:].rearrange("p (a e) -> p a e", a=1).to_broadcast([P, JT, E]),
                            ALU.is_equal)
                    m.then_inc(chosen_ready, 1)
                if live(s - 1):
                    dve.wait_ge(gnn_turned, s)
                    x2 = xs[:, bass.ds((s - 1) * JT, JT), :]
                    dve.tensor_tensor(x2, x2, ps_a[:].rearrange("p (j d) -> p j d", j=JT),
                                      ALU.add).then_inc(x2_ready, 1)
                    wait_apart(dve, x2_ready, s)
                    after(dve, rstd2_ready, s - 1)
                    layer_norm_stats(lambda j: rows_of(s - 1, j), stats2, mv2, var2,
                                     Chain(dve, ln2_chain, (s - 1) * 2)).then_inc(var2_ready, 1)
                if live(s + 1):
                    dve.wait_ge(ms_done, s + 2)
                    after(dve, rrms_ready, s + 1)
                    dve.tensor_scalar(mean_sq[:], ps_c[:, 0:JT], 1.0 / H, RMS_EPS,
                                      ALU.mult, ALU.add).then_inc(ms_ready, 1)
                if live(s - 3):
                    dve.wait_ge(prefix_read, s - 2)
                    ranks.link(dve.tensor_tensor(
                        row_cand[:], row_cand[:], chosen[:, 1 - b, :].rearrange("p (j g) -> p j g", j=JT),
                        ALU.mult))
                    ranks.link(dve.tensor_reduce(
                        row_f[:], row_cand[:].rearrange("p j (k e) -> p (j k) e", k=TOP_K), AX.X, ALU.add))
                    after(dve, dispatched[1 - b], 16 * JT * TOP_K // 2 * (s - 4 + b))
                    dve.wait_ge(tanh_ready, s - 2)
                    mine = (q - 3) % PAYLOADS
                    for k in range(TOP_K):
                        dve.tensor_scalar(payload[:, mine, :, WEIGHT + k], half_tanh[:], 0.5 - k, 0.5,
                                          ALU.mult, ALU.add)
                    dve.tensor_copy(payload[:, mine, :, TOKEN].bitcast(I32), token_no[:])
                    ranks.link(dve.tensor_copy(row_idx[:, 1 - b, :], row_f[:]))
                    dve.tensor_scalar(token_no[:], token_no[:], float(GROUP), None,
                                      ALU.add).then_inc(rows_ready, 1)
                if live(s - 1):
                    dve.wait_ge(rstd2_ready, s)
                    for j in range(JT):
                        m = dve.tensor_scalar(payload[:, (q - 1) % PAYLOADS, j, 0:P], rows_of(s - 1, j),
                                              mv2[:, j, 0:1], rstd2[:, j:j + 1], ALU.subtract, ALU.mult)
                    m.then_inc(xn2_ready, 1)
                if live(s + 1):
                    dve.wait_ge(rrms_ready, s + 2)
                    after(dve, spread_done, s + 1)
                    dve.tensor_tensor(
                        rrms_diag[:], ident[:].rearrange("p (a n) -> p a n", a=1).to_broadcast([P, JT, P]),
                        rrms[:].rearrange("p (j a) -> p j a", a=1).to_broadcast([P, JT, P]),
                        ALU.mult).then_inc(diag_ready, 1)

            dve.wait_ge(dve_consts, 3)
            steps(dve, step, -3, G + 3, 5, G - 3)

            chain = Chain(dve, table_chain, 0)
            dve.wait_ge(rows_ready, G)
            chain.link(dve.tensor_copy(region_end[:], next_row[:]))
            dve.memset(zeros_e[:], 0.0).then_inc(ends_ready, 1)
            chain.link(dve.tensor_tensor(tiles_f[:], next_row[:], region_base[:], ALU.subtract))
            chain.link(dve.tensor_scalar(count_i[:], tiles_f[:], float(SLOTS - 1), None, ALU.add))
            chain.link(dve.tensor_scalar(tiles_i[:], count_i[:], SLOTS.bit_length() - 1, None,
                                         ALU.logical_shift_right))
            chain.link(dve.tensor_copy(tiles_f[:], tiles_i[:]))
            dve.tensor_scalar(skip[:], tiles_f[:], -float(SLOTS), float(REGION), ALU.mult, ALU.add)
            for k in range(TOP_K):
                m = dve.tensor_tensor_scan(tiles_cum[:, k * E:(k + 1) * E], tiles_f[:, k * E:(k + 1) * E],
                                           zeros_e[:], 0.0, ALU.add, ALU.add)
            chain.link(m)
            for k in range(TOP_K):
                ks = slice(k * E, (k + 1) * E)
                tab = slice(k * TILES, (k + 1) * TILES)
                chain.link(dve.tensor_tensor(
                    passed[:], tiles_cum[:, ks].rearrange("p (a e) -> p a e", a=1).to_broadcast([P, TILES, E]),
                    tile_no[:].rearrange("p (i a) -> p i a", a=1).to_broadcast([P, TILES, E]), ALU.is_le))
                dve.tensor_reduce(tile_expert[:], passed[:], AX.X, ALU.add)
                chain.link(dve.tensor_tensor(
                    skipped[:], passed[:],
                    skip[:, ks].rearrange("p (a e) -> p a e", a=1).to_broadcast([P, TILES, E]), ALU.mult))
                chain.link(dve.tensor_reduce(tile_row[:], skipped[:], AX.X, ALU.add))
                chain.link(dve.scalar_tensor_tensor(tile_row[:], tile_no[:], float(SLOTS), tile_row[:],
                                                    ALU.mult, ALU.add))
                chain.link(dve.tensor_scalar(over[:], tile_expert[:], float(E), float(DUMMY),
                                             ALU.is_ge, ALU.mult))
                chain.link(dve.scalar_tensor_tensor(tile_row[:], tile_row[:], float(k * E * REGION), over[:],
                                                    ALU.add, ALU.add))
                dve.tensor_scalar(expert_tab[:, tab], tile_expert[:], float(E - 1), float(BLOCK), ALU.min, ALU.mult)
                chain.link(dve.tensor_scalar(row_tab[:, tab], tile_row[:], float(DUMMY), None, ALU.min))
            dve.wait_ge(experts_loaded, 16 * 3 * E)
            dve.tensor_copy(experts[:].rearrange("p (e w) -> p e w", e=E)[:, :, OB1:OB1 + C],
                            vec_cols[:, FB1:FB1 + E * C].rearrange("p (e c) -> p e c", e=E)
                            ).then_inc(tables_ready, 1)
            dve.wait_ge(tables_ready, 1)

            def copy_block(i, r):
                after(dve, y_done, i - BLOCKS + 1)
                at = dve.value_load(expert_tab[0:1, bass.ds(i, 1)], min_val=0, max_val=(E - 1) * BLOCK)
                dve.tensor_copy(block_w[:, r % BLOCKS, :], experts[:, bass.ds(at, BLOCK)]).then_inc(block_ready, 1)

            def finish(i, r, k):
                y = (ps_b, ps_c)[r % 2]
                dve.wait_ge(y_done, i + 1)
                dve.tensor_tensor(
                    y_bias[:, r % 2, :, :], y[:, 0:SLOTS].rearrange("p (h d) -> p h d", h=HT),
                    block_w[:, r % BLOCKS, OB2:OB2 + P].rearrange("p (a d) -> p a d", a=1).to_broadcast([P, HT, P]),
                    ALU.add).then_inc(y_chain, 1)
                dve.wait_ge(y_chain, i + 1)
                if not isinstance(i, int) or i >= RING:
                    dve.wait_ge(added[r], 16 * HT // RING * (i - r))
                dve.tensor_tensor(y_out[:, r, :, :], y_bias[:, r % 2, :, :],
                                  slot_rows[:, r, :, WEIGHT + k:WEIGHT + k + 1].to_broadcast([P, HT, P]),
                                  ALU.mult).then_inc(y_ready, 1)

            copy_block(0, 0)
            copy_block(1, 1)
            tiles(dve, 0, TILES, lambda i, r: (copy_block(i + 2, (r + 2) % RING), finish(i, r, 0)))
            tiles(dve, TILES, NT - 2, lambda i, r: (copy_block(i + 2, (r + 2) % RING), finish(i, r, 1)))
            finish(NT - 2, (NT - 2) % RING, 1)
            finish(NT - 1, (NT - 1) % RING, 1)


_IN = ["x", "adj_t", "epsilon", "g_w1", "vectors", "g_w2", "f_wg", "f_bg", "f_w1", "f_w2", "f_b2"]


def kernel(x, adj, L0_gnn_epsilon, L0_gnn_W1, L0_gnn_b1, L0_gnn_rms_weight, L0_gnn_W2, L0_gnn_b2,
           L0_ffn_Wg, L0_ffn_bg, L0_ffn_W1, L0_ffn_b1, L0_ffn_W2, L0_ffn_b2):
    import concourse.bacc as bacc
    from concourse.bass_utils import run_bass_kernel_spmd

    B, N, D = x.shape
    E = L0_ffn_Wg.shape[1]
    given = {
        "x": np.asarray(x).reshape(B * N, D),
        "adj_t": np.asarray(adj).transpose(0, 2, 1),
        "epsilon": np.asarray(L0_gnn_epsilon).reshape(1, 1),
        "g_w1": L0_gnn_W1,
        "vectors": np.concatenate([np.asarray(a).reshape(-1, D) for a in
                                   (L0_gnn_b1, L0_gnn_rms_weight, L0_gnn_b2, L0_ffn_b1)]),
        "g_w2": L0_gnn_W2,
        "f_wg": L0_ffn_Wg,
        "f_bg": np.asarray(L0_ffn_bg).reshape(1, E),
        "f_w1": L0_ffn_W1,
        "f_w2": L0_ffn_W2,
        "f_b2": L0_ffn_b2,
    }
    nc = bacc.Bacc("TRN2", target_bir_lowering=False, num_devices=1)
    arrays, args = {}, []
    for name in _IN:
        a = np.ascontiguousarray(given[name])
        arrays[f"in_{name}"] = a
        args.append(nc.dram_tensor(f"in_{name}", a.shape, mybir.dt.from_np(a.dtype), kind="ExternalInput").ap())
    out = nc.dram_tensor("out_y", (B * N, D), F32, kind="ExternalOutput").ap()
    moe_gnn(nc, *args, out)
    r = run_bass_kernel_spmd(nc, [arrays], core_ids=[0])
    return r.results[0]["out_y"].reshape(B, N, D)
```
